# Optimizing a Trainium2 kernel written in Bass

```python
import numpy as np
import jax
import jax.numpy as jnp

def _softmax(x, axis=-1):
    return jax.nn.softmax(x, axis=axis)

def _gelu(x):
    return jax.nn.gelu(x, approximate=True)

def _silu(x):
    return jax.nn.silu(x)

def _sigmoid(x):
    return jax.nn.sigmoid(x)

def _layernorm(x, axis=-1, eps=1e-05):
    m = jnp.mean(x, axis=axis, keepdims=True)
    v = jnp.var(x, axis=axis, keepdims=True)
    return (x - m) / jnp.sqrt(v + eps)

def _scatter_add(tgt, idx, src, axis=0):
    return tgt.at[idx].add(src)

def _segment_sum(src, seg, n):
    return jax.ops.segment_sum(src, seg, n)
kernel_name = 'mk_xattn_seq_d4_seqx_r8_c7eb1f'

def setup_inputs(seed: int=0):
    np.random.seed(seed)
    _w = jnp.asarray

    def _rec_inputs():
        import jax
        import jax.numpy as jnp
        _rk = jax.random.key(seed)
        x = -0.0005146 + 1 * jax.random.normal(jax.random.fold_in(_rk, 1), (4, 256, 256), jnp.float32)
        _lenS = 256 - jax.random.randint(jax.random.fold_in(_rk, 7), (4,), 0, max(1, 256 // 4) + 1, jnp.int32)
        _lenS2 = 256 - jax.random.randint(jax.random.fold_in(_rk, 8), (4,), 0, max(1, 256 // 4) + 1, jnp.int32)
        _ctx_2048P = jax.random.normal(jax.random.fold_in(_rk, 11), (4, 16, 256), jnp.float32)
        _ctx_2048c = jax.random.dirichlet(jax.random.fold_in(_rk, 511), 0.3 * jnp.ones((16,), jnp.float32), (4, 256))
        _ctx_2048t = jnp.einsum('bsk,bkd->bsd', _ctx_2048c, _ctx_2048P)
        _ctx_2048t = _ctx_2048t * jax.lax.rsqrt(jnp.mean(jnp.square(_ctx_2048t)) + 1e-12) * 0.953939
        ctx_2048 = -0.000392918 + 0.999932 * (_ctx_2048t + 0.3 * jax.random.normal(jax.random.fold_in(_rk, 611), (4, 256, 256), jnp.float32))
        _validS = jnp.arange(256)[None, :] < _lenS[:, None]
        _validS2 = jnp.arange(256)[None, :] < _lenS2[:, None]
        _causal = jnp.tril(jnp.ones((256, 256), dtype=bool))
        mask_BxS2_ik0 = jnp.where(jnp.broadcast_to(_validS2[:, :], (4, 256)), 0, 1).astype(jnp.int32)
        mask_1x1xSxS2_fc1 = jnp.where(jnp.broadcast_to(_validS2[0:1, None, None, :], (1, 1, 256, 256)), 1.0, 0.0).astype(jnp.float32)
        mask_Bx1xSxS2_ff1 = jnp.where(jnp.ones((4, 1, 256, 256), dtype=bool), 1.0, 0.0).astype(jnp.float32)
        mask_Bx1xSxS2_ff0 = jnp.where(jnp.ones((4, 1, 256, 256), dtype=bool), 0.0, -1000000000.0).astype(jnp.float32)
        return (x, ctx_2048, mask_BxS2_ik0, mask_1x1xSxS2_fc1, mask_Bx1xSxS2_ff1, mask_Bx1xSxS2_ff0)
    x, ctx_2048, mask_BxS2_ik0, mask_1x1xSxS2_fc1, mask_Bx1xSxS2_ff1, mask_Bx1xSxS2_ff0 = _rec_inputs()

    def _L0_xattn_setup():
        import jax, jax.numpy as jnp
        import numpy as np
        B, P, K, H, NH = (4, 256, 32, 256, 16)
        DH = H // NH
        EPS = 1e-06

        def rmsnorm(x, w):
            var = jnp.mean(jnp.square(x), axis=-1, keepdims=True)
            return x * jax.lax.rsqrt(var + EPS) * w
        key = jax.random.key(seed)
        ks = jax.random.split(key, 12)
        s = 0.02
        return {'x': jax.random.normal(ks[0], (B, P, H), jnp.float32), 'latents': jax.random.normal(ks[1], (B, K, H), jnp.float32), 'attention_mask': jax.random.randint(ks[2], (B, P), 0, 2, jnp.int32), 'q_w': s * jax.random.normal(ks[3], (H, H), jnp.float32), 'q_b': jnp.zeros((H,), jnp.float32), 'kv_w': s * jax.random.normal(ks[4], (H, 2 * H), jnp.float32), 'kv_b': jnp.zeros((2 * H,), jnp.float32), 'out_w': s * jax.random.normal(ks[5], (H, H), jnp.float32), 'out_b': jnp.zeros((H,), jnp.float32), 'postnorm_w': jnp.ones((H,), jnp.float32), 'mlp_w1': s * jax.random.normal(ks[6], (H, 4 * H), jnp.float32), 'mlp_b1': jnp.zeros((4 * H,), jnp.float32), 'mlp_w2': s * jax.random.normal(ks[7], (4 * H, H), jnp.float32), 'mlp_b2': jnp.zeros((H,), jnp.float32)}
    _L0_xattn_all = _L0_xattn_setup()
    _L0_xattn_in = {k: v for k, v in _L0_xattn_all.items() if k in ('q_w', 'q_b', 'kv_w', 'kv_b', 'out_w', 'out_b', 'postnorm_w', 'mlp_w1', 'mlp_b1', 'mlp_w2', 'mlp_b2')}
    del _L0_xattn_all

    def _L1_xattn_setup():
        import jax, jax.numpy as jnp
        import numpy as np
        B, Q, S1, S2 = (4, 32, 256, 256)
        D, H, K, F = (256, 16, 128, 1024)
        LN_EPS = 1e-05

        def _layer_norm(x, scale, offset):
            mu = jnp.mean(x, axis=-1, keepdims=True)
            var = jnp.var(x, axis=-1, keepdims=True)
            return (x - mu) * jax.lax.rsqrt(var + LN_EPS) * scale + offset

        def _cross_attention(q_in, kv_in, wq, bq, wk, bk, wv, bv, wo, bo, bias_k, bias_v):
            b, q_len, _ = q_in.shape
            t = kv_in.shape[1]
            qh = (q_in @ wq + bq).reshape(b, q_len, H, K)
            kh = (kv_in @ wk + bk).reshape(b, t, H, K)
            vh = (kv_in @ wv + bv).reshape(b, t, H, K)
            kh = jnp.concatenate([kh, jnp.broadcast_to(bias_k, (b, 1, H, K))], axis=1)
            vh = jnp.concatenate([vh, jnp.broadcast_to(bias_v, (b, 1, H, K))], axis=1)
            scale = jnp.sqrt(jnp.asarray(K, q_in.dtype))
            logits = jnp.einsum('bqhk,bthk->bhqt', qh, kh) / scale
            weights = jax.nn.softmax(logits, axis=-1)
            ctx = jnp.einsum('bhqt,bthk->bqhk', weights, vh).reshape(b, q_len, H * K)
            return ctx @ wo + bo

        def _forward(x, xf_1, xf_2, ln1_scale, ln1_offset, wq1, bq1, wk1, bk1, wv1, bv1, wo1, bo1, bias_k1, bias_v1, ln2_scale, ln2_offset, wq2, bq2, wk2, bk2, wv2, bv2, wo2, bo2, bias_k2, bias_v2, ln_mlp_scale, ln_mlp_offset, w_fc1, b_fc1, w_fc2, b_fc2):
            res = x
            h = _layer_norm(x, ln1_scale, ln1_offset)
            x = res + _cross_attention(h, xf_1, wq1, bq1, wk1, bk1, wv1, bv1, wo1, bo1, bias_k1, bias_v1)
            res = x
            h = _layer_norm(x, ln2_scale, ln2_offset)
            x = res + _cross_attention(h, xf_2, wq2, bq2, wk2, bk2, wv2, bv2, wo2, bo2, bias_k2, bias_v2)
            h = _layer_norm(x, ln_mlp_scale, ln_mlp_offset)
            h = jax.nn.gelu(h @ w_fc1 + b_fc1, approximate=False) @ w_fc2 + b_fc2
            return x + h
        key = jax.random.key(seed)
        ks = iter(jax.random.split(key, 64))

        def rn(shape, s=0.02):
            return jax.random.normal(next(ks), shape, jnp.float32) * s
        inp = {'x': rn((B, Q, D), 1.0), 'xf_1': rn((B, S1, D), 1.0), 'xf_2': rn((B, S2, D), 1.0)}
        for i in (1, 2):
            inp[f'ln{i}_scale'] = jnp.ones((D,), jnp.float32)
            inp[f'ln{i}_offset'] = jnp.zeros((D,), jnp.float32)
            inp[f'wq{i}'] = rn((D, H * K))
            inp[f'bq{i}'] = jnp.zeros((H * K,), jnp.float32)
            inp[f'wk{i}'] = rn((D, H * K))
            inp[f'bk{i}'] = jnp.zeros((H * K,), jnp.float32)
            inp[f'wv{i}'] = rn((D, H * K))
            inp[f'bv{i}'] = jnp.zeros((H * K,), jnp.float32)
            inp[f'wo{i}'] = rn((H * K, D))
            inp[f'bo{i}'] = jnp.zeros((D,), jnp.float32)
            inp[f'bias_k{i}'] = rn((1, 1, H, K))
            inp[f'bias_v{i}'] = rn((1, 1, H, K))
        inp['ln_mlp_scale'] = jnp.ones((D,), jnp.float32)
        inp['ln_mlp_offset'] = jnp.zeros((D,), jnp.float32)
        inp['w_fc1'] = rn((D, F))
        inp['b_fc1'] = jnp.zeros((F,), jnp.float32)
        inp['w_fc2'] = rn((F, D))
        inp['b_fc2'] = jnp.zeros((D,), jnp.float32)
        return inp
    _L1_xattn_all = _L1_xattn_setup()
    _L1_xattn_in = {k: v for k, v in _L1_xattn_all.items() if k in ('ln1_scale', 'ln1_offset', 'wq1', 'bq1', 'wk1', 'bk1', 'wv1', 'bv1', 'wo1', 'bo1', 'bias_k1', 'bias_v1', 'ln2_scale', 'ln2_offset', 'wq2', 'bq2', 'wk2', 'bk2', 'wv2', 'bv2', 'wo2', 'bo2', 'bias_k2', 'bias_v2', 'ln_mlp_scale', 'ln_mlp_offset', 'w_fc1', 'b_fc1', 'w_fc2', 'b_fc2')}
    del _L1_xattn_all

    def _L2_xattn_setup():
        import jax, jax.numpy as jnp
        import numpy as np
        H = 256
        NH = 16
        HD = H // NH
        EPS = 1e-05

        def gelu(x):
            return 0.5 * x * (1.0 + jnp.tanh(0.7978845608028654 * x * (1.0 + 0.044715 * x * x)))

        def layernorm(x, scale, bias):
            m = jnp.mean(x, axis=-1, keepdims=True)
            v = jnp.mean(jnp.square(x - m), axis=-1, keepdims=True)
            return (x - m) * jax.lax.rsqrt(v + EPS) * scale + bias

        def split_heads(x):
            b, s, _ = x.shape
            return x.reshape(b, s, NH, HD).transpose(0, 2, 1, 3)

        def merge_heads(x):
            b, nh, s, hd = x.shape
            return x.transpose(0, 2, 1, 3).reshape(b, s, nh * hd)

        def attention(q, k, v, mask):
            scores = jnp.einsum('bhqd,bhkd->bhqk', q, k) / jnp.sqrt(jnp.float32(HD))
            scores = scores * mask - 10000.0 * (1.0 - mask)
            probs = jax.nn.softmax(scores, axis=-1)
            return jnp.einsum('bhqk,bhkd->bhqd', probs, v)
        key = jax.random.key(seed)
        ks = jax.random.split(key, 16)
        b, s, t = (2, 128, 128)
        w = lambda k, i, o: jax.random.normal(k, (i, o), jnp.float32) * 0.02
        inp = {'hidden_states': jax.random.normal(ks[0], (b, s, H), jnp.float32), 'encoder_states': jax.random.normal(ks[1], (b, t, H), jnp.float32), 'ltor_mask': jnp.tril(jnp.ones((1, 1, s, s), jnp.float32)), 'cross_mask': jnp.ones((b, 1, s, t), jnp.float32), 'ln1_s': jnp.ones((H,), jnp.float32), 'ln1_b': jnp.zeros((H,), jnp.float32), 'w_qkv': w(ks[2], H, 3 * H), 'b_qkv': jnp.zeros((3 * H,), jnp.float32), 'w_ao': w(ks[3], H, H), 'b_ao': jnp.zeros((H,), jnp.float32), 'ln2_s': jnp.ones((H,), jnp.float32), 'ln2_b': jnp.zeros((H,), jnp.float32), 'w_q': w(ks[4], H, H), 'b_q': jnp.zeros((H,), jnp.float32), 'w_kv': w(ks[5], H, 2 * H), 'b_kv': jnp.zeros((2 * H,), jnp.float32), 'w_co': w(ks[6], H, H), 'b_co': jnp.zeros((H,), jnp.float32), 'ln3_s': jnp.ones((H,), jnp.float32), 'ln3_b': jnp.zeros((H,), jnp.float32), 'w1': w(ks[7], H, 4 * H), 'b1': jnp.zeros((4 * H,), jnp.float32), 'w2': w(ks[8], 4 * H, H), 'b2': jnp.zeros((H,), jnp.float32)}
        return inp
    _L2_xattn_all = _L2_xattn_setup()
    _L2_xattn_in = {k: v for k, v in _L2_xattn_all.items() if k in ('ln1_s', 'ln1_b', 'w_qkv', 'b_qkv', 'w_ao', 'b_ao', 'ln2_s', 'ln2_b', 'w_q', 'b_q', 'w_kv', 'b_kv', 'w_co', 'b_co', 'ln3_s', 'ln3_b', 'w1', 'b1', 'w2', 'b2')}
    del _L2_xattn_all

    def _L3_xattn_setup():
        import jax, jax.numpy as jnp
        import numpy as np
        H = 256
        NH = 32
        KVH = 8
        HD = H // NH
        GROUPS = NH // KVH
        EPS = 1e-06
        B, L, S = (4, 128, 128)

        def _gqa_forward(hidden_state, encoder_hidden_state, encoder_attention_mask, Wq, bq, Wk, bk, Wv, bv, Wo, bo, gamma, beta):
            b, l, _ = hidden_state.shape
            s = encoder_hidden_state.shape[1]
            q = hidden_state @ Wq + bq
            k = encoder_hidden_state @ Wk + bk
            v = encoder_hidden_state @ Wv + bv
            q = q.reshape(b, l, KVH, GROUPS, HD).transpose(0, 2, 3, 1, 4)
            k = k.reshape(b, s, KVH, HD).transpose(0, 2, 1, 3)
            v = v.reshape(b, s, KVH, HD).transpose(0, 2, 1, 3)
            scale = 1.0 / jnp.sqrt(jnp.asarray(HD, q.dtype))
            scores = jnp.einsum('bkgld,bksd->bkgls', q, k) * scale
            scores = scores + encoder_attention_mask[:, :, None, :, :]
            attn = jax.nn.softmax(scores, axis=-1)
            out = jnp.einsum('bkgls,bksd->bkgld', attn, v)
            out = out.transpose(0, 3, 1, 2, 4).reshape(b, l, H)
            out = out @ Wo + bo
            x = out + hidden_state
            mu = jnp.mean(x, axis=-1, keepdims=True)
            var = jnp.var(x, axis=-1, keepdims=True)
            return (x - mu) * jax.lax.rsqrt(var + EPS) * gamma + beta
        key = jax.random.key(seed)
        ks = jax.random.split(key, 12)
        sd = 0.02
        return {'hidden_state': jax.random.normal(ks[0], (B, L, H), jnp.float32), 'encoder_hidden_state': jax.random.normal(ks[1], (B, S, H), jnp.float32), 'encoder_attention_mask': jnp.zeros((B, 1, L, S), jnp.float32), 'Wq': jax.random.normal(ks[2], (H, H), jnp.float32) * sd, 'bq': jnp.zeros((H,), jnp.float32), 'Wk': jax.random.normal(ks[3], (H, KVH * HD), jnp.float32) * sd, 'bk': jnp.zeros((KVH * HD,), jnp.float32), 'Wv': jax.random.normal(ks[4], (H, KVH * HD), jnp.float32) * sd, 'bv': jnp.zeros((KVH * HD,), jnp.float32), 'Wo': jax.random.normal(ks[5], (H, H), jnp.float32) * sd, 'bo': jnp.zeros((H,), jnp.float32), 'gamma': jnp.ones((H,), jnp.float32), 'beta': jnp.zeros((H,), jnp.float32)}
    _L3_xattn_all = _L3_xattn_setup()
    _L3_xattn_in = {k: v for k, v in _L3_xattn_all.items() if k in ('Wq', 'bq', 'Wk', 'bk', 'Wv', 'bv', 'Wo', 'bo', 'gamma', 'beta')}
    del _L3_xattn_all
    return {'x': x, 'ctx_2048': ctx_2048, 'mask_BxS2_ik0': mask_BxS2_ik0, 'mask_1x1xSxS2_fc1': mask_1x1xSxS2_fc1, 'mask_Bx1xSxS2_ff1': mask_Bx1xSxS2_ff1, 'mask_Bx1xSxS2_ff0': mask_Bx1xSxS2_ff0, 'L0_xattn_q_w': _L0_xattn_in['q_w'], 'L0_xattn_q_b': _L0_xattn_in['q_b'], 'L0_xattn_kv_w': _L0_xattn_in['kv_w'], 'L0_xattn_kv_b': _L0_xattn_in['kv_b'], 'L0_xattn_out_w': _L0_xattn_in['out_w'], 'L0_xattn_out_b': _L0_xattn_in['out_b'], 'L0_xattn_postnorm_w': _L0_xattn_in['postnorm_w'], 'L0_xattn_mlp_w1': _L0_xattn_in['mlp_w1'], 'L0_xattn_mlp_b1': _L0_xattn_in['mlp_b1'], 'L0_xattn_mlp_w2': _L0_xattn_in['mlp_w2'], 'L0_xattn_mlp_b2': _L0_xattn_in['mlp_b2'], 'L1_xattn_ln1_scale': _L1_xattn_in['ln1_scale'], 'L1_xattn_ln1_offset': _L1_xattn_in['ln1_offset'], 'L1_xattn_wq1': _L1_xattn_in['wq1'], 'L1_xattn_bq1': _L1_xattn_in['bq1'], 'L1_xattn_wk1': _L1_xattn_in['wk1'], 'L1_xattn_bk1': _L1_xattn_in['bk1'], 'L1_xattn_wv1': _L1_xattn_in['wv1'], 'L1_xattn_bv1': _L1_xattn_in['bv1'], 'L1_xattn_wo1': _L1_xattn_in['wo1'], 'L1_xattn_bo1': _L1_xattn_in['bo1'], 'L1_xattn_bias_k1': _L1_xattn_in['bias_k1'], 'L1_xattn_bias_v1': _L1_xattn_in['bias_v1'], 'L1_xattn_ln2_scale': _L1_xattn_in['ln2_scale'], 'L1_xattn_ln2_offset': _L1_xattn_in['ln2_offset'], 'L1_xattn_wq2': _L1_xattn_in['wq2'], 'L1_xattn_bq2': _L1_xattn_in['bq2'], 'L1_xattn_wk2': _L1_xattn_in['wk2'], 'L1_xattn_bk2': _L1_xattn_in['bk2'], 'L1_xattn_wv2': _L1_xattn_in['wv2'], 'L1_xattn_bv2': _L1_xattn_in['bv2'], 'L1_xattn_wo2': _L1_xattn_in['wo2'], 'L1_xattn_bo2': _L1_xattn_in['bo2'], 'L1_xattn_bias_k2': _L1_xattn_in['bias_k2'], 'L1_xattn_bias_v2': _L1_xattn_in['bias_v2'], 'L1_xattn_ln_mlp_scale': _L1_xattn_in['ln_mlp_scale'], 'L1_xattn_ln_mlp_offset': _L1_xattn_in['ln_mlp_offset'], 'L1_xattn_w_fc1': _L1_xattn_in['w_fc1'], 'L1_xattn_b_fc1': _L1_xattn_in['b_fc1'], 'L1_xattn_w_fc2': _L1_xattn_in['w_fc2'], 'L1_xattn_b_fc2': _L1_xattn_in['b_fc2'], 'L2_xattn_ln1_s': _L2_xattn_in['ln1_s'], 'L2_xattn_ln1_b': _L2_xattn_in['ln1_b'], 'L2_xattn_w_qkv': _L2_xattn_in['w_qkv'], 'L2_xattn_b_qkv': _L2_xattn_in['b_qkv'], 'L2_xattn_w_ao': _L2_xattn_in['w_ao'], 'L2_xattn_b_ao': _L2_xattn_in['b_ao'], 'L2_xattn_ln2_s': _L2_xattn_in['ln2_s'], 'L2_xattn_ln2_b': _L2_xattn_in['ln2_b'], 'L2_xattn_w_q': _L2_xattn_in['w_q'], 'L2_xattn_b_q': _L2_xattn_in['b_q'], 'L2_xattn_w_kv': _L2_xattn_in['w_kv'], 'L2_xattn_b_kv': _L2_xattn_in['b_kv'], 'L2_xattn_w_co': _L2_xattn_in['w_co'], 'L2_xattn_b_co': _L2_xattn_in['b_co'], 'L2_xattn_ln3_s': _L2_xattn_in['ln3_s'], 'L2_xattn_ln3_b': _L2_xattn_in['ln3_b'], 'L2_xattn_w1': _L2_xattn_in['w1'], 'L2_xattn_b1': _L2_xattn_in['b1'], 'L2_xattn_w2': _L2_xattn_in['w2'], 'L2_xattn_b2': _L2_xattn_in['b2'], 'L3_xattn_Wq': _L3_xattn_in['Wq'], 'L3_xattn_bq': _L3_xattn_in['bq'], 'L3_xattn_Wk': _L3_xattn_in['Wk'], 'L3_xattn_bk': _L3_xattn_in['bk'], 'L3_xattn_Wv': _L3_xattn_in['Wv'], 'L3_xattn_bv': _L3_xattn_in['bv'], 'L3_xattn_Wo': _L3_xattn_in['Wo'], 'L3_xattn_bo': _L3_xattn_in['bo'], 'L3_xattn_gamma': _L3_xattn_in['gamma'], 'L3_xattn_beta': _L3_xattn_in['beta']}

def reference(x, ctx_2048, mask_BxS2_ik0, mask_1x1xSxS2_fc1, mask_Bx1xSxS2_ff1, mask_Bx1xSxS2_ff0, L0_xattn_q_w, L0_xattn_q_b, L0_xattn_kv_w, L0_xattn_kv_b, L0_xattn_out_w, L0_xattn_out_b, L0_xattn_postnorm_w, L0_xattn_mlp_w1, L0_xattn_mlp_b1, L0_xattn_mlp_w2, L0_xattn_mlp_b2, L1_xattn_ln1_scale, L1_xattn_ln1_offset, L1_xattn_wq1, L1_xattn_bq1, L1_xattn_wk1, L1_xattn_bk1, L1_xattn_wv1, L1_xattn_bv1, L1_xattn_wo1, L1_xattn_bo1, L1_xattn_bias_k1, L1_xattn_bias_v1, L1_xattn_ln2_scale, L1_xattn_ln2_offset, L1_xattn_wq2, L1_xattn_bq2, L1_xattn_wk2, L1_xattn_bk2, L1_xattn_wv2, L1_xattn_bv2, L1_xattn_wo2, L1_xattn_bo2, L1_xattn_bias_k2, L1_xattn_bias_v2, L1_xattn_ln_mlp_scale, L1_xattn_ln_mlp_offset, L1_xattn_w_fc1, L1_xattn_b_fc1, L1_xattn_w_fc2, L1_xattn_b_fc2, L2_xattn_ln1_s, L2_xattn_ln1_b, L2_xattn_w_qkv, L2_xattn_b_qkv, L2_xattn_w_ao, L2_xattn_b_ao, L2_xattn_ln2_s, L2_xattn_ln2_b, L2_xattn_w_q, L2_xattn_b_q, L2_xattn_w_kv, L2_xattn_b_kv, L2_xattn_w_co, L2_xattn_b_co, L2_xattn_ln3_s, L2_xattn_ln3_b, L2_xattn_w1, L2_xattn_b1, L2_xattn_w2, L2_xattn_b2, L3_xattn_Wq, L3_xattn_bq, L3_xattn_Wk, L3_xattn_bk, L3_xattn_Wv, L3_xattn_bv, L3_xattn_Wo, L3_xattn_bo, L3_xattn_gamma, L3_xattn_beta):
    import jax
    import jax.numpy as jnp

    def _L0_xattn_ref(x, latents, attention_mask, q_w, q_b, kv_w, kv_b, out_w, out_b, postnorm_w, mlp_w1, mlp_b1, mlp_w2, mlp_b2):
        import jax, jax.numpy as jnp
        import numpy as np
        B, P, K, H, NH = (4, 256, 32, 256, 16)
        DH = H // NH
        EPS = 1e-06

        def rmsnorm(x, w):
            var = jnp.mean(jnp.square(x), axis=-1, keepdims=True)
            return x * jax.lax.rsqrt(var + EPS) * w
        b, p, _ = x.shape
        k_len = latents.shape[1]
        residual = latents
        h = jnp.concatenate([x, latents], axis=1)
        q = (latents @ q_w + q_b).reshape(b, k_len, NH, DH)
        kv = (h @ kv_w + kv_b).reshape(b, p + k_len, NH, DH, 2)
        kmat, v = (kv[..., 0], kv[..., 1])
        attn = jnp.einsum('bkhd,bnhd->bhkn', q, kmat) / DH
        full_mask = jnp.concatenate([attention_mask.astype(bool), jnp.ones((b, k_len), bool)], axis=-1)
        attn = jnp.where(full_mask[:, None, None, :], attn, -jnp.inf)
        attn = jax.nn.softmax(attn.astype(jnp.float32), axis=-1).astype(q.dtype)
        attn_out = jnp.einsum('bhkn,bnhd->bkhd', attn, v).reshape(b, k_len, H)
        attn_out = attn_out @ out_w + out_b + residual
        out = rmsnorm(attn_out, postnorm_w)
        out = jax.nn.gelu(out @ mlp_w1 + mlp_b1) @ mlp_w2 + mlp_b2
        return out + residual

    def _L1_xattn_ref(x, xf_1, xf_2, ln1_scale, ln1_offset, wq1, bq1, wk1, bk1, wv1, bv1, wo1, bo1, bias_k1, bias_v1, ln2_scale, ln2_offset, wq2, bq2, wk2, bk2, wv2, bv2, wo2, bo2, bias_k2, bias_v2, ln_mlp_scale, ln_mlp_offset, w_fc1, b_fc1, w_fc2, b_fc2):
        import jax, jax.numpy as jnp
        import numpy as np
        B, Q, S1, S2 = (4, 32, 256, 256)
        D, H, K, F = (256, 16, 128, 1024)
        LN_EPS = 1e-05

        def _layer_norm(x, scale, offset):
            mu = jnp.mean(x, axis=-1, keepdims=True)
            var = jnp.var(x, axis=-1, keepdims=True)
            return (x - mu) * jax.lax.rsqrt(var + LN_EPS) * scale + offset

        def _cross_attention(q_in, kv_in, wq, bq, wk, bk, wv, bv, wo, bo, bias_k, bias_v):
            b, q_len, _ = q_in.shape
            t = kv_in.shape[1]
            qh = (q_in @ wq + bq).reshape(b, q_len, H, K)
            kh = (kv_in @ wk + bk).reshape(b, t, H, K)
            vh = (kv_in @ wv + bv).reshape(b, t, H, K)
            kh = jnp.concatenate([kh, jnp.broadcast_to(bias_k, (b, 1, H, K))], axis=1)
            vh = jnp.concatenate([vh, jnp.broadcast_to(bias_v, (b, 1, H, K))], axis=1)
            scale = jnp.sqrt(jnp.asarray(K, q_in.dtype))
            logits = jnp.einsum('bqhk,bthk->bhqt', qh, kh) / scale
            weights = jax.nn.softmax(logits, axis=-1)
            ctx = jnp.einsum('bhqt,bthk->bqhk', weights, vh).reshape(b, q_len, H * K)
            return ctx @ wo + bo

        def _forward(x, xf_1, xf_2, ln1_scale, ln1_offset, wq1, bq1, wk1, bk1, wv1, bv1, wo1, bo1, bias_k1, bias_v1, ln2_scale, ln2_offset, wq2, bq2, wk2, bk2, wv2, bv2, wo2, bo2, bias_k2, bias_v2, ln_mlp_scale, ln_mlp_offset, w_fc1, b_fc1, w_fc2, b_fc2):
            res = x
            h = _layer_norm(x, ln1_scale, ln1_offset)
            x = res + _cross_attention(h, xf_1, wq1, bq1, wk1, bk1, wv1, bv1, wo1, bo1, bias_k1, bias_v1)
            res = x
            h = _layer_norm(x, ln2_scale, ln2_offset)
            x = res + _cross_attention(h, xf_2, wq2, bq2, wk2, bk2, wv2, bv2, wo2, bo2, bias_k2, bias_v2)
            h = _layer_norm(x, ln_mlp_scale, ln_mlp_offset)
            h = jax.nn.gelu(h @ w_fc1 + b_fc1, approximate=False) @ w_fc2 + b_fc2
            return x + h
        return _forward(x, xf_1, xf_2, ln1_scale, ln1_offset, wq1, bq1, wk1, bk1, wv1, bv1, wo1, bo1, bias_k1, bias_v1, ln2_scale, ln2_offset, wq2, bq2, wk2, bk2, wv2, bv2, wo2, bo2, bias_k2, bias_v2, ln_mlp_scale, ln_mlp_offset, w_fc1, b_fc1, w_fc2, b_fc2)

    def _L2_xattn_ref(hidden_states, encoder_states, ltor_mask, cross_mask, ln1_s, ln1_b, w_qkv, b_qkv, w_ao, b_ao, ln2_s, ln2_b, w_q, b_q, w_kv, b_kv, w_co, b_co, ln3_s, ln3_b, w1, b1, w2, b2):
        import jax, jax.numpy as jnp
        import numpy as np
        H = 256
        NH = 16
        HD = H // NH
        EPS = 1e-05

        def gelu(x):
            return 0.5 * x * (1.0 + jnp.tanh(0.7978845608028654 * x * (1.0 + 0.044715 * x * x)))

        def layernorm(x, scale, bias):
            m = jnp.mean(x, axis=-1, keepdims=True)
            v = jnp.mean(jnp.square(x - m), axis=-1, keepdims=True)
            return (x - m) * jax.lax.rsqrt(v + EPS) * scale + bias

        def split_heads(x):
            b, s, _ = x.shape
            return x.reshape(b, s, NH, HD).transpose(0, 2, 1, 3)

        def merge_heads(x):
            b, nh, s, hd = x.shape
            return x.transpose(0, 2, 1, 3).reshape(b, s, nh * hd)

        def attention(q, k, v, mask):
            scores = jnp.einsum('bhqd,bhkd->bhqk', q, k) / jnp.sqrt(jnp.float32(HD))
            scores = scores * mask - 10000.0 * (1.0 - mask)
            probs = jax.nn.softmax(scores, axis=-1)
            return jnp.einsum('bhqk,bhkd->bhqd', probs, v)
        ln_out = layernorm(hidden_states, ln1_s, ln1_b)
        qkv = ln_out @ w_qkv + b_qkv
        q, k, v = jnp.split(qkv, 3, axis=-1)
        ctx = merge_heads(attention(split_heads(q), split_heads(k), split_heads(v), ltor_mask))
        attn_out = ctx @ w_ao + b_ao
        x = hidden_states + attn_out
        ln_out = layernorm(x, ln2_s, ln2_b)
        q = ln_out @ w_q + b_q
        kv = encoder_states @ w_kv + b_kv
        k, v = jnp.split(kv, 2, axis=-1)
        ctx = merge_heads(attention(split_heads(q), split_heads(k), split_heads(v), cross_mask))
        cross_out = ctx @ w_co + b_co
        x = x + cross_out
        ln_out = layernorm(x, ln3_s, ln3_b)
        mlp_out = gelu(ln_out @ w1 + b1) @ w2 + b2
        return x + mlp_out

    def _L3_xattn_ref(hidden_state, encoder_hidden_state, encoder_attention_mask, Wq, bq, Wk, bk, Wv, bv, Wo, bo, gamma, beta):
        import jax, jax.numpy as jnp
        import numpy as np
        H = 256
        NH = 32
        KVH = 8
        HD = H // NH
        GROUPS = NH // KVH
        EPS = 1e-06
        B, L, S = (4, 128, 128)

        def _gqa_forward(hidden_state, encoder_hidden_state, encoder_attention_mask, Wq, bq, Wk, bk, Wv, bv, Wo, bo, gamma, beta):
            b, l, _ = hidden_state.shape
            s = encoder_hidden_state.shape[1]
            q = hidden_state @ Wq + bq
            k = encoder_hidden_state @ Wk + bk
            v = encoder_hidden_state @ Wv + bv
            q = q.reshape(b, l, KVH, GROUPS, HD).transpose(0, 2, 3, 1, 4)
            k = k.reshape(b, s, KVH, HD).transpose(0, 2, 1, 3)
            v = v.reshape(b, s, KVH, HD).transpose(0, 2, 1, 3)
            scale = 1.0 / jnp.sqrt(jnp.asarray(HD, q.dtype))
            scores = jnp.einsum('bkgld,bksd->bkgls', q, k) * scale
            scores = scores + encoder_attention_mask[:, :, None, :, :]
            attn = jax.nn.softmax(scores, axis=-1)
            out = jnp.einsum('bkgls,bksd->bkgld', attn, v)
            out = out.transpose(0, 3, 1, 2, 4).reshape(b, l, H)
            out = out @ Wo + bo
            x = out + hidden_state
            mu = jnp.mean(x, axis=-1, keepdims=True)
            var = jnp.var(x, axis=-1, keepdims=True)
            return (x - mu) * jax.lax.rsqrt(var + EPS) * gamma + beta
        return _gqa_forward(hidden_state, encoder_hidden_state, encoder_attention_mask, Wq, bq, Wk, bk, Wv, bv, Wo, bo, gamma, beta)
    x = _L0_xattn_ref(ctx_2048, x, mask_BxS2_ik0, L0_xattn_q_w, L0_xattn_q_b, L0_xattn_kv_w, L0_xattn_kv_b, L0_xattn_out_w, L0_xattn_out_b, L0_xattn_postnorm_w, L0_xattn_mlp_w1, L0_xattn_mlp_b1, L0_xattn_mlp_w2, L0_xattn_mlp_b2)
    x = _L1_xattn_ref(x, ctx_2048, ctx_2048, L1_xattn_ln1_scale, L1_xattn_ln1_offset, L1_xattn_wq1, L1_xattn_bq1, L1_xattn_wk1, L1_xattn_bk1, L1_xattn_wv1, L1_xattn_bv1, L1_xattn_wo1, L1_xattn_bo1, L1_xattn_bias_k1, L1_xattn_bias_v1, L1_xattn_ln2_scale, L1_xattn_ln2_offset, L1_xattn_wq2, L1_xattn_bq2, L1_xattn_wk2, L1_xattn_bk2, L1_xattn_wv2, L1_xattn_bv2, L1_xattn_wo2, L1_xattn_bo2, L1_xattn_bias_k2, L1_xattn_bias_v2, L1_xattn_ln_mlp_scale, L1_xattn_ln_mlp_offset, L1_xattn_w_fc1, L1_xattn_b_fc1, L1_xattn_w_fc2, L1_xattn_b_fc2)
    x = _L2_xattn_ref(x, ctx_2048, mask_1x1xSxS2_fc1, mask_Bx1xSxS2_ff1, L2_xattn_ln1_s, L2_xattn_ln1_b, L2_xattn_w_qkv, L2_xattn_b_qkv, L2_xattn_w_ao, L2_xattn_b_ao, L2_xattn_ln2_s, L2_xattn_ln2_b, L2_xattn_w_q, L2_xattn_b_q, L2_xattn_w_kv, L2_xattn_b_kv, L2_xattn_w_co, L2_xattn_b_co, L2_xattn_ln3_s, L2_xattn_ln3_b, L2_xattn_w1, L2_xattn_b1, L2_xattn_w2, L2_xattn_b2)
    x = _L3_xattn_ref(x, ctx_2048, mask_Bx1xSxS2_ff0, L3_xattn_Wq, L3_xattn_bq, L3_xattn_Wk, L3_xattn_bk, L3_xattn_Wv, L3_xattn_bv, L3_xattn_Wo, L3_xattn_bo, L3_xattn_gamma, L3_xattn_beta)
    return x

_drawn_inputs = setup_inputs


def setup_inputs(seed=0):
    import zlib

    import numpy as np

    out = dict(_drawn_inputs(seed))
    spreads = {'L0_xattn_q_b': (0.0, 0.8),
     'L0_xattn_kv_b': (0.0, 0.8),
     'L0_xattn_out_b': (0.0, 0.712),
     'L0_xattn_postnorm_w': (1.0, 0.6),
     'L0_xattn_mlp_b1': (0.0, 0.1),
     'L0_xattn_mlp_b2': (0.0, 0.1),
     'L1_xattn_ln1_scale': (1.0, 0.6),
     'L1_xattn_ln1_offset': (0.0, 0.8),
     'L1_xattn_bq1': (0.0, 0.8),
     'L1_xattn_bk1': (0.0, 2.0),
     'L1_xattn_bv1': (0.0, 0.1),
     'L1_xattn_bo1': (0.0, 0.1),
     'L1_xattn_ln2_scale': (1.0, 0.6),
     'L1_xattn_ln2_offset': (0.0, 0.8),
     'L1_xattn_bq2': (0.0, 0.8),
     'L1_xattn_bk2': (0.0, 2.0),
     'L1_xattn_bv2': (0.0, 0.1),
     'L1_xattn_bo2': (0.0, 0.1),
     'L1_xattn_ln_mlp_scale': (1.0, 0.6),
     'L1_xattn_ln_mlp_offset': (0.0, 0.7),
     'L1_xattn_b_fc1': (0.0, 0.1),
     'L1_xattn_b_fc2': (0.0, 0.1),
     'L2_xattn_ln1_s': (1.0, 0.6),
     'L2_xattn_ln1_b': (0.0, 0.8),
     'L2_xattn_b_qkv': (0.0, 0.294),
     'L2_xattn_b_ao': (0.0, 0.1),
     'L2_xattn_ln2_s': (1.0, 0.6),
     'L2_xattn_ln2_b': (0.0, 2.0),
     'L2_xattn_b_q': (0.0, 2.0),
     'L2_xattn_b_kv': (0.0, 0.274),
     'L2_xattn_b_co': (0.0, 0.1),
     'L2_xattn_ln3_s': (1.0, 0.6),
     'L2_xattn_ln3_b': (0.0, 0.694),
     'L2_xattn_b1': (0.0, 0.1),
     'L2_xattn_b2': (0.0, 0.1),
     'L3_xattn_bq': (0.0, 0.8),
     'L3_xattn_bk': (0.0, 2.0),
     'L3_xattn_bv': (0.0, 0.291),
     'L3_xattn_bo': (0.0, 0.1),
     'L3_xattn_gamma': (1.0, 0.2),
     'L3_xattn_beta': (0.0, 0.1)}
    factors = {'L0_xattn_q_w': 8.0,
     'L0_xattn_kv_w': 8.0,
     'L0_xattn_out_w': 8.0,
     'L1_xattn_wq1': 8.0,
     'L1_xattn_wk1': 8.0,
     'L1_xattn_bias_k1': 64.0,
     'L1_xattn_bias_v1': 64.0,
     'L1_xattn_wq2': 8.0,
     'L1_xattn_wk2': 8.0,
     'L1_xattn_bias_k2': 64.0,
     'L1_xattn_bias_v2': 64.0,
     'L2_xattn_w_q': 8.0,
     'L3_xattn_Wq': 8.0,
     'L3_xattn_Wk': 8.0}
    for name, (base, spread) in spreads.items():
        noise = np.random.default_rng([zlib.crc32(name.encode()), seed]).standard_normal(out[name].shape)
        drawn = base * np.exp(spread * noise) if base else spread * noise
        out[name] = jnp.asarray(drawn.astype(out[name].dtype))
    for name, factor in factors.items():
        out[name] = (out[name] * factor).astype(out[name].dtype)
    return out
```

```python
from contextlib import ExitStack

import concourse.bass as bass
from concourse import mybir

ALU = mybir.AluOpType
ACT = mybir.ActivationFunctionType
AX = mybir.AxisListType
F32 = mybir.dt.float32
I32 = mybir.dt.int32

P = 128
B = 4
T = 256
D = 256
KT = D // P
QT = T // P
F = 4 * D
FT = F // P
SLOT = 32
QUAD = P // SLOT
LAG = 3
PROBS = 4
BIG = -1.0e30
LOWEST = -3.0e38
KQ_BANK = [2, 2, 3, 2]
V_BANK = [3, 4]
G1, H1 = 4, 4
K1 = T + 1

COLS = ["q0", "k0", "b10", "post", "ln1s", "ln1o", "ln2s", "ln2o", "lnms", "lnmo", "b11",
        "l2s1", "l2b1", "q2", "k2", "l2s2", "l2b2", "q2c", "k2c", "l2s3", "l2b3", "b12", "q3", "k3",
        "bq1", "bk1", "key1", "bq2", "bk2", "key2"]
WIDTHS = dict.fromkeys(COLS, KT) | dict.fromkeys(["b10", "b11", "b12"], FT) | {"k3": 1} | dict.fromkeys(
    ["bq1", "bk1", "key1", "bq2", "bk2", "key2"], G1 * H1)
ROWS = ["v0", "o0", "m0", "o1", "o2", "m1", "v2", "o2s", "v2c", "o2c", "m2", "v3", "o3", "gamma", "beta"]
COL_AT = {n: sum(WIDTHS[m] for m in COLS[:i]) for i, n in enumerate(COLS)}
NCOL = sum(WIDTHS.values())


class Tally:

    def __init__(self, base, per):
        self.base, self.per = {n: base.get(n, 1) for n in per}, per

    def at(self, name, turn, k=0):
        return turn * self.per[name] + (self.base[name] + k)

    def since(self, name, turn, k):
        return self.at(name, turn, max(k, 0))


def small(name, **k):
    wide = dict(name=name, heads=16, dh=16, kv=KT, kinds="mult", qcol="q" + name, kcol="k" + name,
                head=lambda h: (h // 8, h % 8, h // 8, h), ktiles=2, marks="m16", vheads=16)
    return wide | k


SMALL = [
    small("0", kv=4, kinds="add", scale=1.0 / 16, vrow="v0", orow="o0", w=0, first="x"),
    small("2", scale=0.25, vrow="v2", orow="o2s", w=1, self_kv=True),
    small("2c", scale=0.25, vrow="v2c", orow="o2c", w=0),
    small("3", heads=32, dh=8, kinds="add", scale=8.0 ** -0.5, vrow="v3", orow="o3", w=1, marks="m8",
          vheads=8, ktiles=1,
          head=lambda h: (h % 4 // 2, h % 2 * 8 + h // 4, 0, h // 4)),
]


def build(nc, a):
    ctx = ExitStack()
    with ctx:
        def sb(name, shape, dt=F32):
            return ctx.enter_context(nc.sbuf_tensor(name, shape, dt))

        sems = {}

        def sem(name):
            if name not in sems:
                sems[name] = ctx.enter_context(nc.semaphore(name))
            return sems[name]

        bank = [ctx.enter_context(nc.psum_tensor(f"bank{i}", [P, 512], F32)) for i in range(8)]

        x_rows = sb("x_rows", [P, B * QT, D])
        y_rows = sb("y_rows", [P, B * QT, D])
        hT = sb("hT", [P, B, KT, T])
        ident = sb("ident", [P, P])
        marks = {"m16": sb("m16", [P, 8]), "m8": sb("m8", [P, 16])}
        cols = sb("cols", [P, NCOL])
        rows = sb("rows", [P, len(ROWS), D])
        half = sb("half", [P, QT])
        w_qkv = [sb(f"w_qkv{i}", [P, 3, KT, D]) for i in range(2)]
        w_o = [sb("w_o0", [P, 4, D]), sb("w_o1", [P, 8, D])]
        w_m1 = sb("w_m1", [P, KT, F])
        w_m2 = sb("w_m2", [P, FT, D])
        g_qkv = sb("g_qkv", [P, 3, KT, H1 * P])
        g_o = sb("g_o", [P, H1, D])
        g_bv = sb("g_bv", [P, H1 * P])
        g_key_v = sb("g_key_v", [P, H1, G1 * H1])
        kvT = sb("kvT", [P, KT, 2 * T])
        mask_i = sb("mask_i", [P, T], I32)
        mask_m = sb("mask_m", [P, QT * T])
        mask_a = sb("mask_a", [P, QT * T])
        qT = sb("qT", [P, KT, T])
        q_one = sb("q_one", [P, 4, T])
        kT = sb("kT", [P, 2, 2 * T])
        v_sb = sb("v_sb", [P, 4, 16, SLOT])
        probs = sb("probs", [P, PROBS, QT, 2 * T])
        pT = sb("pT", [P, 6, 4, T])
        oT = sb("oT", [P, 8, T])
        stats = sb("stats", [P, PROBS, 2, QT])
        sums = sb("sums", [P, 2, QT, QUAD])
        recips = sb("recips", [P, 2, QT * QUAD, SLOT])
        recip = sb("recip", [P, QT, QUAD])
        recipT = sb("recipT", [P, T])
        kT1 = sb("kT1", [P, 2, K1])
        qT1 = sb("qT1", [P, 2, T])
        v1 = sb("v1", [P, QT, H1 * P])
        probs1 = sb("probs1", [P, 2, QT, K1])
        pT1 = sb("pT1", [P, 2, QT, T])
        oT1 = sb("oT1", [P, H1, T])
        stats1 = sb("stats1", [P, 2, 4, QT])
        p_key = sb("p_key", [P, B * QT, G1 * H1])
        p_keyT = sb("p_keyT", [G1 * H1, T])
        p_key_b = sb("p_key_b", [P, QT, G1 * H1])
        key_out = sb("key_out", [G1 * H1, D])
        h1T = pT[:, 0:2, :, :].rearrange("p a t q -> p (a t) q")
        z = sb("z", [P, QT, D])
        bn = sb("bn", [P, QT, 6])
        mv = sb("mv", [P, QT, 2])
        ms = sb("ms", [P, QT])
        rstd = sb("rstd", [P, QT])

        def col(name, i):
            return cols[:, COL_AT[name] + i:COL_AT[name] + i + 1]

        def row(name):
            return rows[:, ROWS.index(name), :]

        def row2(name):
            return rows[:, ROWS.index(name):ROWS.index(name) + 1, :].to_broadcast([P, QT, D])

        base = {}
        def stage(turns, per):
            t = Tally(base, per)
            for n, v in per.items():
                base[n] = base.get(n, 1) + turns * v
            return t

        def small_stage(c):
            nq, nh = c["heads"] // QUAD, c["heads"]
            return stage(B, dict(
                a_loaded={"0": 32, "2": 0, "2c": 16, "3": 16}[c["name"]], a_maskin=0 if c["name"] == "2" else 16,
                a_kv=int("self_kv" in c), a_mask=1, a_proj=5 if c["kv"] == 4 else 3, a_qout=KT,
                a_kout=c["ktiles"], a_vout=c["kv"], a_qone=nh, a_scores=nh,
                a_masked=nh if c["kinds"] == "mult" else 0, a_max=nh, a_negmax=nh, a_exp=nh, a_inv=nq, a_recip=nq,
                a_t=nh, a_tout=nh, a_pv=nq, a_rout=nq, a_oout=nq, a_y=1, a_resid=1, a_yout=1))

        def norm_stage(kind):
            n, turned = int(kind != "raw"), int(kind != "last")
            return stage(B, dict(l_bn=n, l_mv=n, l_ms=n, l_eps=n, l_rstd=n, l_z=1, l_t=turned, l_h=turned,
                                 l_gam=1 - turned, l_out=1 - turned, l_store=16 * (1 - turned)))

        def mlp_stage():
            return stage(B, dict(m_h=FT, m_gelu=FT, m_y=1, m_resid=1, m_out=1))

        def wide_stage():
            return stage(G1 * B, dict(b_loaded=16, b_proj=6, b_kq=4, b_v=2, b_scores=2 * H1, b_rmax=2 * H1, b_negmax=H1,
                                      b_exp=2 * H1, b_recip=H1, b_probs=H1, b_t=H1, b_tout=H1, b_pv=H1,
                                      b_oout=H1, b_y=1, b_yout=1))

        def group_stage():
            return stage(G1, dict(c_qkv=16, c_bv=16, c_o=32, c_key=1, c_keyout=1))

        def key_stage():
            return stage(B, dict(d_copy=1, d_t=1, d_tout=1, d_y=1, d_yout=1))

        S = {}
        S["a0"] = small_stage(SMALL[0])
        S["l0"] = norm_stage("rms")
        S["m0"] = mlp_stage()
        for j in (1, 2):
            S[f"l1{j}"] = norm_stage("ln")
            S[f"g1{j}"] = group_stage()
            S[f"b1{j}"] = wide_stage()
            S[f"d1{j}"] = key_stage()
        S["l1m"] = norm_stage("ln")
        S["m1"] = mlp_stage()
        S["l21"] = norm_stage("ln")
        S["a2"] = small_stage(SMALL[1])
        S["l22"] = norm_stage("ln")
        S["a2c"] = small_stage(SMALL[2])
        S["l23"] = norm_stage("ln")
        S["m2"] = mlp_stage()
        S["l3t"] = norm_stage("raw")
        S["a3"] = small_stage(SMALL[3])
        S["l3"] = norm_stage("last")

        def end(st, name, turns=B):
            return S[st].base[name] + turns * S[st].per[name]

        block = ctx.enter_context(nc.Block())

        @block.sync
        def _(sp):
            def load(dst, src, name):
                sp.dma_start(dst, src).then_inc(sem(name), 16)

            load(ident[:, :], a["ident"], "s_const")
            load(marks["m16"][:, :], a["m16"], "s_const")
            load(marks["m8"][:, :], a["m8"], "s_const")
            load(cols[:, :], a["cols"], "s_const")
            load(hT[:, :, :, :], a["xT"].rearrange("b p k t -> p b k t"), "s_const")
            load(w_qkv[0][:, :, :, :], a["w_0"], "s_w0")
            load(w_o[0][:, :, :], a["wo_0"], "s_w0")
            load(rows[:, :, :].rearrange("p r d -> p (r d)"), a["rows"].to_broadcast([P, len(ROWS) * D]), "s_const")
            load(x_rows[:, :, :], a["x"], "s_const")

            for name in sorted(base):
                sp.sem_inc(sem(name), 1)

            def mlp_weights(n):
                load(w_m1[:, :, :], a[f"w1_{n}"], "s_wm")
                load(w_m2[:, :, :], a[f"w2_{n}"], "s_wm")

            def small_loads(c):
                st = S["a" + c["name"]]
                with sp.Fori(0, B) as b:
                    if "self_kv" not in c:
                        sp.wait_ge(sem("a_proj"), st.at("a_proj", b))
                        load(kvT[:, :, 0:T], a["ctxT"][b], "a_loaded")
                    if c["name"] == "0":
                        load(kvT[:, :, T:2 * T], a["xT"][b], "a_loaded")
                        sp.wait_ge(sem("a_mask"), st.at("a_mask", b))
                        load(mask_i[:, :], a["mask"][b].to_broadcast([P, T]), "a_maskin")
                    elif c["name"] != "2":
                        sp.wait_ge(sem("a_max"), st.at("a_max", b))
                        load(mask_m[:, :], a["mask_" + c["name"]][b], "a_maskin")

            mlp_weights(0)
            small_loads(SMALL[0])
            sp.wait_ge(sem("a_proj"), end("a0", "a_proj"))
            for j in (1, 2):
                gs, bs = S[f"g1{j}"], S[f"b1{j}"]
                with sp.Fori(0, G1) as g:
                    sp.wait_ge(sem("b_proj"), bs.at("b_proj", g * B))
                    load(g_qkv[:, :, :, :], a[f"g{j}"][g], "c_qkv")
                    load(kvT[:, :, 0:T], a["ctxT"][0], "b_loaded")
                    sp.wait_ge(sem("b_v"), bs.at("b_v", g * B))
                    load(g_bv[:, :], a[f"gbv{j}"][g].to_broadcast([P, H1 * P]), "c_bv")
                    sp.wait_ge(sem("c_key"), gs.at("c_key", g))
                    load(g_o[:, :, :], a[f"go{j}"][g], "c_o")
                    load(g_key_v[:, :, :], a[f"gkey{j}"][g], "c_o")
                    with sp.Fori(1, B) as b:
                        sp.wait_ge(sem("b_proj"), bs.at("b_proj", g * B + b))
                        load(kvT[:, :, 0:T], a["ctxT"][b], "b_loaded")
                if j == 1:
                    sp.wait_ge(sem("m_y"), end("m0", "m_y"))
                    mlp_weights(1)
                    load(w_qkv[1][:, :, :, :], a["w_2"], "s_w1")
                    load(w_o[1][:, 0:4, :], a["wo_2"], "s_w1")
                    sp.wait_ge(sem("a_y"), end("a0", "a_y"))
                    load(w_qkv[0][:, :, :, :], a["w_2c"], "s_w0")
                    load(w_o[0][:, :, :], a["wo_2c"], "s_w0")
            sp.wait_ge(sem("a_max"), end("a0", "a_max"))
            load(mask_m[:, :], a["mask_2"], "s_m2")
            small_loads(SMALL[1])
            sp.wait_ge(sem("m_y"), end("m1", "m_y"))
            mlp_weights(2)
            sp.wait_ge(sem("a_y"), end("a2", "a_y"))
            load(w_qkv[1][:, :, :, :], a["w_3"], "s_w1")
            load(w_o[1][:, :, :], a["wo_3"], "s_w1")
            small_loads(SMALL[2])
            small_loads(SMALL[3])
            st = S["l3"]
            with sp.Fori(0, B) as b:
                sp.wait_ge(sem("l_out"), st.at("l_out", b, 1))
                sp.dma_start(a["out"][b], z[:, :, :]).then_inc(sem("l_store"), 16)
            sp.wait_ge(sem("l_store"), end("l3", "l_store"))

        @block.tensor
        def _(pe):
            mm = nc.tensor.matmul

            def norm(name):
                st = S[name]
                with pe.Fori(0, B) as b:
                    pe.wait_ge(sem("l_z"), st.at("l_z", b, 1))
                    pe.wait_ge(sem("l_h"), st.at("l_h", b))
                    for q in range(QT):
                        for k in range(KT):
                            last = nc.tensor.transpose(bank[0][:, k * T + q * P:k * T + (q + 1) * P],
                                                       z[:, q, k * P:(k + 1) * P], ident[:, :])
                    last.then_inc(sem("l_t"), 1)

            def attention(c, wn):
                st = S["a" + c["name"]]
                w, wo = w_qkv[c["w"]], w_o[c["w"]]
                nh, nkv = c["heads"], c["kv"]
                vw = c["vheads"] * c["dh"]
                pe.wait_ge(sem(f"s_w{c['w']}"), wn)
                with pe.Fori(0, B) as b:
                    pe.wait_ge(sem("a_max"), st.at("a_max", b))
                    pe.wait_ge(sem("a_yout"), st.at("a_yout", b))
                    if "self_kv" in c:
                        pe.wait_ge(sem("a_kv"), st.at("a_kv", b, 1))
                    else:
                        pe.wait_ge(sem("a_loaded"), st.at("a_loaded", b, st.per["a_loaded"]))
                    for i in range(KT):
                        for k in range(KT):
                            last = mm(bank[0][:, i * T:(i + 1) * T], w[:, 0, k, i * P:(i + 1) * P],
                                      hT[:, b, k, :], start=(k == 0), stop=(k == KT - 1))
                    last.then_inc(sem("a_proj"), 1)
                    n = 1
                    for i in range(c["ktiles"]):
                        if nkv == 4:
                            out = bank[n][:, :]
                        else:
                            out = bank[n][:, i * T:(i + 1) * T]
                        for k in range(KT):
                            last = mm(out, w[:, 1, k, i * P:(i + 1) * P], kvT[:, k, 0:nkv * P],
                                      start=(k == 0), stop=(k == KT - 1))
                        if nkv == 4 or i == c["ktiles"] - 1:
                            last.then_inc(sem("a_proj"), 1)
                            n += 1
                    for t in range(nkv):
                        vb = [bank[3], bank[7]][t // 2]
                        for k in range(KT):
                            last = mm(vb[:, t % 2 * T:t % 2 * T + vw], kvT[:, k, t * P:(t + 1) * P],
                                      w[:, 2, k, 0:vw], start=(k == 0), stop=(k == KT - 1))
                        if t % 2:
                            last.then_inc(sem("a_proj"), 1)

                    def scores(h):
                        pe.wait_ge(sem("a_qone"), st.at("a_qone", b, h + 1))
                        kt_ = c["head"](h)[2]
                        if h == 0:
                            pe.wait_ge(sem("a_kout"), st.at("a_kout", b, st.per["a_kout"]))
                            pe.wait_ge(sem("a_vout"), st.at("a_vout", b, st.per["a_vout"]))
                        lag = 2 if nkv == 4 else 4
                        if h >= lag:
                            free = "a_masked" if c["kinds"] == "mult" else "a_max"
                            pe.wait_ge(sem(free), st.at(free, b, h - lag + 1))
                        for q in range(QT):
                            out = bank[h % 2 * 2 + q][:, :] if nkv == 4 else bank[h % 4][:, q * T:(q + 1) * T]
                            last = mm(out, q_one[:, h % 4, q * P:(q + 1) * P], kT[:, kt_, 0:nkv * P],
                                      start=True, stop=True)
                        last.then_inc(sem("a_scores"), 1)

                    def transposes(h):
                        pe.wait_ge(sem("a_exp"), st.at("a_exp", b, h + 1))
                        lag = 1 if nkv == 4 else 2
                        pe.wait_ge(sem("a_tout"), st.since("a_tout", b, h - lag + 1))
                        for t in range(nkv):
                            tb = bank[4 + t // 2] if nkv == 4 else bank[4 + h % 2]
                            for q in range(QT):
                                last = nc.tensor.transpose(tb[:, t % 2 * T + q * P:t % 2 * T + (q + 1) * P],
                                                           probs[:, h % PROBS, q, t * P:(t + 1) * P], ident[:, :])
                        last.then_inc(sem("a_t"), 1)

                    def outputs(g):
                        pe.wait_ge(sem("a_tout"), st.at("a_tout", b, QUAD * (g + 1)))
                        pe.wait_ge(sem("a_oout"), st.since("a_oout", b, g))
                        for t in range(nkv):
                            for j in range(QUAD):
                                h = QUAD * g + j
                                last = mm(bank[6][SLOT * j:SLOT * (j + 1), 0:T],
                                          v_sb[:, t, c["head"](h)[3], :], pT[:, h % 6, t, :],
                                          start=(t == 0), stop=(t == nkv - 1), skip_group_check=True)
                        pe.wait_ge(sem("a_recip"), st.at("a_recip", b, g + 1))
                        for q in range(QT):
                            r = recips[:, g % 2, q * QUAD:(q + 1) * QUAD, :].rearrange("p j s -> p (j s)")
                            last = nc.tensor.transpose(bank[6][:, T + q * P:T + (q + 1) * P], r, ident[:, :])
                        last.then_inc(sem("a_pv"), 1)

                    for i in range(nh + QUAD + 1):
                        if i < nh:
                            scores(i)
                        if LAG <= i < nh + LAG:
                            transposes(i - LAG)
                        if i >= 2 * QUAD and i % QUAD == 0:
                            outputs(i // QUAD - 2)
                    ng = nh // QUAD
                    pe.wait_ge(sem("a_oout"), st.at("a_oout", b, ng))
                    for q in range(QT):
                        for g in range(ng):
                            last = mm(bank[7][:, q * D:(q + 1) * D], oT[:, g, q * P:(q + 1) * P], wo[:, g, :],
                                      start=(g == 0), stop=(g == ng - 1))
                    last.then_inc(sem("a_y"), 1)

            def mlp(n):
                st = S[f"m{n}"]
                pe.wait_ge(sem("s_wm"), 32 * (n + 1))
                with pe.Fori(0, B) as b:
                    for f in range(FT + 2):
                        if f < FT:
                            pe.wait_ge(sem("m_gelu"), st.since("m_gelu", b, f - 3))
                            for k in range(KT):
                                last = mm(bank[f % 4][:, 0:T], w_m1[:, k, f * P:(f + 1) * P],
                                          hT[:, b, k, :], start=(k == 0), stop=(k == KT - 1))
                            last.then_inc(sem("m_h"), 1)
                        if f >= 2:
                            if f == 2:
                                pe.wait_ge(sem("m_out"), st.at("m_out", b))
                            pe.wait_ge(sem("m_gelu"), st.at("m_gelu", b, f - 1))
                            for q in range(QT):
                                last = mm(bank[6 + q][:, 0:D], h1T[:, f - 2, q * P:(q + 1) * P],
                                          w_m2[:, f - 2, :], start=(f == 2), stop=(f == FT + 1))
                    last.then_inc(sem("m_y"), 1)

            def wide(j):
                gs, st = S[f"g1{j}"], S[f"b1{j}"]
                with pe.Fori(0, G1) as g:
                    with pe.Fori(0, B) as b:
                        u = g * B + b
                        pe.wait_ge(sem("c_qkv"), gs.at("c_qkv", g, 16))
                        pe.wait_ge(sem("b_loaded"), st.at("b_loaded", u, 16))

                        def kq(h):
                            out = bank[KQ_BANK[h]]
                            if h == 0:
                                pe.wait_ge(sem("b_kq"), st.at("b_kq", u))
                            elif h == 1:
                                pe.wait_ge(sem("b_kq"), st.at("b_kq", u, 1))
                            elif h == 2:
                                pe.wait_ge(sem("b_v"), st.at("b_v", u, 1))
                            else:
                                pe.wait_ge(sem("b_kq"), st.at("b_kq", u, 2))
                            for k in range(KT):
                                mm(out[:, 0:T], g_qkv[:, 1, k, h * P:(h + 1) * P], kvT[:, k, 0:T],
                                   start=(k == 0), stop=(k == KT - 1))
                            for k in range(KT):
                                last = mm(out[:, T:2 * T], g_qkv[:, 0, k, h * P:(h + 1) * P], hT[:, b, k, :],
                                          start=(k == 0), stop=(k == KT - 1))
                            last.then_inc(sem("b_proj"), 1)

                        def values(t):
                            if t == 1:
                                pe.wait_ge(sem("b_tout"), st.at("b_tout", u))
                            for k in range(KT):
                                last = mm(bank[V_BANK[t]][:, :], kvT[:, k, t * P:(t + 1) * P], g_qkv[:, 2, k, :],
                                          start=(k == 0), stop=(k == KT - 1))
                            last.then_inc(sem("b_proj"), 1)

                        def scores(h):
                            pe.wait_ge(sem("b_kq"), st.at("b_kq", u, h + 1))
                            for q in range(QT):
                                pe.wait_ge(sem("b_exp"), st.since("b_exp", u, 2 * (h - 1) + q + 1))
                                mm(bank[q][:, 0:K1], qT1[:, h % 2, q * P:(q + 1) * P], kT1[:, h % 2, :],
                                   start=True, stop=True).then_inc(sem("b_scores"), 1)

                        def transposes(h):
                            pe.wait_ge(sem("b_probs"), st.at("b_probs", u, h + 1))
                            pe.wait_ge(sem("b_tout"), st.at("b_tout", u, h))
                            if h == 0:
                                pe.wait_ge(sem("b_v"), st.at("b_v", u, 2))
                            for t in range(QT):
                                for q in range(QT):
                                    last = nc.tensor.transpose(bank[4][:, t * T + q * P:t * T + (q + 1) * P],
                                                               probs1[:, h % 2, q, t * P:(t + 1) * P], ident[:, :])
                            last.then_inc(sem("b_t"), 1)

                        def outputs(h):
                            if h == 0:
                                pe.wait_ge(sem("b_v"), st.at("b_v", u, 2))
                            pe.wait_ge(sem("b_tout"), st.at("b_tout", u, h + 1))
                            pe.wait_ge(sem("b_oout"), st.at("b_oout", u, h))
                            for t in range(QT):
                                last = mm(bank[6][:, 0:T], v1[:, t, h * P:(h + 1) * P], pT1[:, h % 2, t, :],
                                          start=(t == 0), stop=(t == QT - 1))
                            last.then_inc(sem("b_pv"), 1)

                        def project(h):
                            pe.wait_ge(sem("b_oout"), st.at("b_oout", u, h + 1))
                            if h == 0:
                                pe.wait_ge(sem("b_yout"), st.at("b_yout", u))
                                pe.wait_ge(sem("c_keyout"), gs.at("c_keyout", g))
                                pe.wait_ge(sem("c_o"), gs.at("c_o", g, 32))
                            for q in range(QT):
                                last = mm(bank[[5, 7][q]][:, 0:D], oT1[:, h, q * P:(q + 1) * P], g_o[:, h, :],
                                          start=(h == 0), stop=(h == H1 - 1))
                            if h == H1 - 1:
                                last.then_inc(sem("b_y"), 1)

                        kq(0)
                        values(0)
                        values(1)
                        scores(0)
                        kq(1)
                        kq(2)
                        scores(1)
                        transposes(0)
                        kq(3)
                        outputs(0)
                        scores(2)
                        transposes(1)
                        project(0)
                        outputs(1)
                        scores(3)
                        transposes(2)
                        project(1)
                        outputs(2)
                        transposes(3)
                        project(2)
                        outputs(3)
                        project(3)
                    pe.wait_ge(sem("b_yout"), st.at("b_yout", (g + 1) * B))
                    for h in range(H1):
                        last = mm(bank[7][0:G1 * H1, 0:D], g_key_v[:, h, :], g_o[:, h, :],
                                  start=(h == 0), stop=(h == H1 - 1))
                    last.then_inc(sem("c_key"), 1)

            def learned_key(j):
                st = S[f"d1{j}"]
                pe.wait_ge(sem("c_keyout"), end(f"g1{j}", "c_keyout", G1))
                pe.wait_ge(sem("b_yout"), end(f"b1{j}", "b_yout", G1 * B))
                with pe.Fori(0, B) as b:
                    pe.wait_ge(sem("d_copy"), st.at("d_copy", b, 1))
                    pe.wait_ge(sem("d_tout"), st.at("d_tout", b))
                    for q in range(QT):
                        last = nc.tensor.transpose(bank[4][0:G1 * H1, q * P:(q + 1) * P], p_key_b[:, q, :], ident[:, :])
                    last.then_inc(sem("d_t"), 1)
                    pe.wait_ge(sem("d_tout"), st.at("d_tout", b, 1))
                    pe.wait_ge(sem("d_yout"), st.at("d_yout", b))
                    for q in range(QT):
                        last = mm(bank[7][:, q * D:(q + 1) * D], p_keyT[:, q * P:(q + 1) * P], key_out[:, :],
                                  start=True, stop=True)
                    last.then_inc(sem("d_y"), 1)

            pe.wait_ge(sem("s_const"), 112)
            attention(SMALL[0], 32)
            norm("l0")
            pe.wait_ge(sem("l_h"), end("l0", "l_h"))
            mlp(0)
            for j in (1, 2):
                norm(f"l1{j}")
                pe.wait_ge(sem("l_h"), end(f"l1{j}", "l_h"))
                wide(j)
                learned_key(j)
            norm("l1m")
            pe.wait_ge(sem("l_h"), end("l1m", "l_h"))
            mlp(1)
            norm("l21")
            pe.wait_ge(sem("l_h"), end("l21", "l_h"))
            attention(SMALL[1], 32)
            norm("l22")
            pe.wait_ge(sem("l_h"), end("l22", "l_h"))
            attention(SMALL[2], 64)
            norm("l23")
            pe.wait_ge(sem("l_h"), end("l23", "l_h"))
            mlp(2)
            norm("l3t")
            pe.wait_ge(sem("l_h"), end("l3t", "l_h"))
            attention(SMALL[3], 64)


        @block.scalar
        def _(act):
            def norm(name, scale=None, offset=None):
                st = S[name]
                with act.Fori(0, B) as b:
                    act.wait_ge(sem("l_t"), st.at("l_t", b, 1))
                    for k in range(KT):
                        last = nc.scalar.activation(hT[:, b, k, :], bank[0][:, k * T:(k + 1) * T], ACT.Identity,
                                                    bias=col(offset, k) if offset else 0.0,
                                                    scale=col(scale, k) if scale else 1.0)
                    last.then_inc(sem("l_h"), 1)

            def attention(c):
                st = S["a" + c["name"]]
                nh, nkv = c["heads"], c["kv"]
                with act.Fori(0, B) as b:
                    for i in range(c["ktiles"]):
                        act.wait_ge(sem("a_proj"), st.at("a_proj", b, 2 + i if nkv == 4 else 2))
                        if i == 0:
                            act.wait_ge(sem("a_scores"), st.at("a_scores", b))
                        src = bank[1 + i][:, :] if nkv == 4 else bank[1][:, i * T:(i + 1) * T]
                        nc.scalar.activation(kT[:, i, 0:nkv * P], src, ACT.Identity,
                                             bias=col(c["kcol"], i)).then_inc(sem("a_kout"), 1)
                    for i in range(nh + LAG):
                        if i >= LAG:
                            h = i - LAG
                            act.wait_ge(sem("a_t"), st.at("a_t", b, h + 1))
                            act.wait_ge(sem("a_pv"), st.since("a_pv", b, (h - 6) // QUAD + 1))
                            for t in range(0, nkv, 2):
                                tb = bank[4 + t // 2] if nkv == 4 else bank[4 + h % 2]
                                last = nc.scalar.activation(pT[:, h % 6, t:t + 2, :].rearrange("p t q -> p (t q)"),
                                                            tb[:, :], ACT.Copy)
                            last.then_inc(sem("a_tout"), 1)
                        if i < nh:
                            act.wait_ge(sem("a_negmax"), st.at("a_negmax", b, i + 1))
                            if i % QUAD == 0:
                                act.wait_ge(sem("a_recip"), st.since("a_recip", b, i // QUAD - 1))
                            for q in range(QT):
                                s = probs[:, i % PROBS, q, 0:nkv * P]
                                last = nc.scalar.activation(s, s, ACT.Exp, bias=stats[:, i % PROBS, 1, q:q + 1],
                                                            scale=c["scale"], accum_out=sums[:, i // QUAD % 2, q, i % QUAD:i % QUAD + 1])
                            last.then_inc(sem("a_exp"), 1)

            def mlp(n, gelu):
                st = S[f"m{n}"]
                with act.Fori(0, B) as b:
                    act.wait_ge(sem("m_y"), st.at("m_y", b))
                    for f in range(FT):
                        act.wait_ge(sem("m_h"), st.at("m_h", b, f + 1))
                        nc.scalar.activation(h1T[:, f, :], bank[f % 4][:, 0:T], gelu,
                                             bias=col(f"b1{n}", f)).then_inc(sem("m_gelu"), 1)

            def wide(j):
                st = S[f"b1{j}"]
                scale = P ** -0.5
                with act.Fori(0, G1) as g:
                    with act.Fori(0, B) as b:
                        u = g * B + b

                        def kq(h):
                            act.wait_ge(sem("b_proj"), st.at("b_proj", u, [1, 4, 5, 6][h]))
                            act.wait_ge(sem("b_scores"), st.since("b_scores", u, 2 * (h - 1)))
                            src = bank[KQ_BANK[h]]
                            nc.scalar.activation(kT1[:, h % 2, 0:T], src[:, 0:T], ACT.Identity,
                                                 bias=cols[:, bass.ds(g * H1 + (COL_AT[f"bk{j}"] + h), 1)])
                            nc.scalar.activation(kT1[:, h % 2, T:K1], cols[:, bass.ds(g * H1 + (COL_AT[f"key{j}"] + h), 1)],
                                                 ACT.Copy)
                            nc.scalar.activation(qT1[:, h % 2, :], src[:, T:2 * T], ACT.Identity,
                                                 bias=cols[:, bass.ds(g * H1 + (COL_AT[f"bq{j}"] + h), 1)])\
                                .then_inc(sem("b_kq"), 1)

                        def exps(h):
                            act.wait_ge(sem("b_t"), st.since("b_t", u, h - 1))
                            act.wait_ge(sem("b_negmax"), st.at("b_negmax", u, h + 1))
                            for q in range(QT):
                                nc.scalar.activation(probs1[:, h % 2, q, :], bank[q][:, 0:K1], ACT.Exp,
                                                     bias=stats1[:, h % 2, 1, q:q + 1], scale=scale,
                                                     accum_out=stats1[:, h % 2, 2, q:q + 1]).then_inc(sem("b_exp"), 1)

                        def turned(h):
                            act.wait_ge(sem("b_t"), st.at("b_t", u, h + 1))
                            act.wait_ge(sem("b_pv"), st.since("b_pv", u, h - 1))
                            nc.scalar.activation(pT1[:, h % 2, :, :].rearrange("p t q -> p (t q)"), bank[4][:, :],
                                                 ACT.Copy).then_inc(sem("b_tout"), 1)

                        kq(0)
                        exps(0)
                        kq(1)
                        kq(2)
                        exps(1)
                        turned(0)
                        kq(3)
                        exps(2)
                        turned(1)
                        exps(3)
                        turned(2)
                        turned(3)

            def learned_key(j):
                st = S[f"d1{j}"]
                with act.Fori(0, B) as b:
                    act.wait_ge(sem("d_t"), st.at("d_t", b, 1))
                    act.wait_ge(sem("d_y"), st.at("d_y", b))
                    nc.scalar.activation(p_keyT[:, :], bank[4][0:G1 * H1, 0:T], ACT.Copy).then_inc(sem("d_tout"), 1)

            act.wait_ge(sem("s_const"), 112)
            attention(SMALL[0])
            norm("l0", "post")
            mlp(0, ACT.Gelu_apprx_tanh)
            for j in (1, 2):
                norm(f"l1{j}", f"ln{j}s", f"ln{j}o")
                wide(j)
                learned_key(j)
            norm("l1m", "lnms", "lnmo")
            mlp(1, ACT.Gelu)
            norm("l21", "l2s1", "l2b1")
            attention(SMALL[1])
            norm("l22", "l2s2", "l2b2")
            attention(SMALL[2])
            norm("l23", "l2s3", "l2b3")
            mlp(2, ACT.Gelu_apprx_tanh)
            norm("l3t")
            attention(SMALL[3])

        def plain_wait(dve):
            dve.sem_inc(sem("e_step"), 1)

        @block.vector
        def _(dve):
            v = nc.vector

            def norm(name, kind, src, eps=0.0):
                st = S[name]
                with dve.Fori(0, B) as b:
                    xs = src[:, bass.ds(b * QT, QT), :]
                    if kind == "last":
                        dve.wait_ge(sem("l_store"), st.at("l_store", b))
                    else:
                        dve.wait_ge(sem("l_t"), st.at("l_t", b))
                    if kind == "raw":
                        v.tensor_copy(z[:, :, :], xs).then_inc(sem("l_z"), 1)
                    else:
                        for q in range(QT):
                            last = v.bn_stats(bn[:, q, :], src[:, b * QT + q, :])
                        last.then_inc(sem("l_bn"), 1)
                        dve.wait_ge(sem("l_bn"), st.at("l_bn", b, 1))
                        plain_wait(dve)
                        for q in range(QT):
                            last = v.bn_aggr(mv[:, q, :], bn[:, q, :])
                        last.then_inc(sem("l_mv"), 1)
                        dve.wait_ge(sem("l_mv"), st.at("l_mv", b, 1))
                        if kind == "rms":
                            v.tensor_tensor(ms[:, :], mv[:, :, 0], mv[:, :, 0], ALU.mult).then_inc(sem("l_ms"), 1)
                            dve.wait_ge(sem("l_ms"), st.at("l_ms", b, 1))
                            v.scalar_tensor_tensor(ms[:, :], ms[:, :], eps, mv[:, :, 1], ALU.add, ALU.add)\
                                .then_inc(sem("l_eps"), 1)
                        else:
                            v.tensor_scalar(ms[:, :], mv[:, :, 1], eps, None, ALU.add).then_inc(sem("l_eps"), 1)
                            dve.sem_inc(sem("l_ms"), 1)
                        dve.wait_ge(sem("l_rstd"), st.at("l_rstd", b, 1))
                        for q in range(QT):
                            xq = src[:, b * QT + q, :]
                            if kind == "rms":
                                last = v.tensor_scalar(z[:, q, :], xq, rstd[:, q:q + 1], None, ALU.mult)
                            else:
                                last = v.tensor_scalar(z[:, q, :], xq, mv[:, q, 0:1], rstd[:, q:q + 1],
                                                       ALU.subtract, ALU.mult)
                        last.then_inc(sem("l_z"), 1)
                        if kind == "last":
                            dve.wait_ge(sem("l_z"), st.at("l_z", b, 1))
                            v.tensor_tensor(z[:, :, :], z[:, :, :], row2("gamma"), ALU.mult).then_inc(sem("l_gam"), 1)
                            dve.wait_ge(sem("l_gam"), st.at("l_gam", b, 1))
                            v.tensor_tensor(z[:, :, :], z[:, :, :], row2("beta"), ALU.add).then_inc(sem("l_out"), 1)

            def attention(c, dst):
                st = S["a" + c["name"]]
                nh, nkv, dh = c["heads"], c["kv"], c["dh"]
                v.memset(v_sb[:, :, :, dh:SLOT], 0.0)
                if c["name"] == "0":
                    v.memset(mask_a[:, T:2 * T], 0.0)
                if c["name"] == "2":
                    dve.wait_ge(sem("s_m2"), 16)
                with dve.Fori(0, B) as b:
                    xs = x_rows[:, bass.ds(b * QT, QT), :]
                    ys = dst[:, bass.ds(b * QT, QT), :]
                    if "self_kv" in c:
                        dve.wait_ge(sem("a_proj"), st.at("a_proj", b))
                        v.tensor_copy(kvT[:, :, 0:T], hT[:, b, :, :]).then_inc(sem("a_kv"), 1)
                    if st.per["a_maskin"]:
                        dve.wait_ge(sem("a_maskin"), st.at("a_maskin", b, 16))
                    if c["name"] == "0":
                        ins = v.tensor_scalar(mask_a[:, 0:T], mask_i[:, :], 0.0, BIG, ALU.is_equal, ALU.mult)
                    elif c["kinds"] == "mult":
                        ins = v.tensor_scalar(mask_a[:, :], mask_m[:, :], -1.0, 10000.0 / c["scale"],
                                              ALU.add, ALU.mult)
                    else:
                        ins = v.tensor_scalar(mask_a[:, :], mask_m[:, :], 1.0 / c["scale"], None, ALU.mult)
                    ins.then_inc(sem("a_mask"), 1)
                    dve.wait_ge(sem("a_proj"), st.at("a_proj", b, 1))
                    for i in range(KT):
                        if i == 0:
                            dve.wait_ge(sem("a_qone"), st.at("a_qone", b))
                        v.tensor_scalar(qT[:, i, :], bank[0][:, i * T:(i + 1) * T], col(c["qcol"], i), None,
                                        ALU.add).then_inc(sem("a_qout"), 1)

                    for t in range(nkv):
                        if t % 2 == 0:
                            dve.wait_ge(sem("a_proj"), st.at("a_proj", b, st.per["a_proj"] - nkv // 2 + t // 2 + 1))
                        vw = c["vheads"] * dh
                        v.tensor_tensor(
                            v_sb[:, t, 0:c["vheads"], 0:dh],
                            [bank[3], bank[7]][t // 2][:, t % 2 * T:t % 2 * T + vw].rearrange("p (h d) -> p h d", d=dh),
                            row(c["vrow"])[:, 0:vw].rearrange("p (h d) -> p h d", d=dh),
                            ALU.add).then_inc(sem("a_vout"), 1)
                    v.tensor_tensor(ys, xs, row2(c["orow"]), ALU.add).then_inc(sem("a_resid"), 1)

                    def times_mask(h):
                        dve.wait_ge(sem("a_scores"), st.at("a_scores", b, h + 1))
                        if h >= PROBS:
                            dve.wait_ge(sem("a_t"), st.at("a_t", b, h - PROBS + 1))
                        v.tensor_tensor(probs[:, h % PROBS, :, 0:T],
                                        bank[h % 4][:, :].rearrange("p (q t) -> p q t", q=QT),
                                        mask_m[:, :].rearrange("p (q t) -> p q t", q=QT),
                                        ALU.mult).then_inc(sem("a_masked"), 1)

                    def maxima(h):
                        if c["kinds"] == "mult":
                            dve.wait_ge(sem("a_masked"), st.at("a_masked", b, h + 1))
                        else:
                            dve.wait_ge(sem("a_scores"), st.at("a_scores", b, h + 1))
                            if h >= PROBS:
                                dve.wait_ge(sem("a_t"), st.at("a_t", b, h - PROBS + 1))
                        if h == 0:
                            dve.wait_ge(sem("a_mask"), st.at("a_mask", b, 1))
                        plain_wait(dve)
                        for q in range(QT):
                            if nkv == 4:
                                src, add = bank[h % 2 * 2 + q][:, :], mask_a[:, :]
                            else:
                                src, add = bank[h % 4][:, q * T:(q + 1) * T], mask_a[:, q * T:(q + 1) * T]
                            if c["kinds"] == "mult":
                                src = probs[:, h % PROBS, q, 0:T]
                            last = v.tensor_tensor_reduce(probs[:, h % PROBS, q, 0:nkv * P], src, add, 1.0, LOWEST,
                                                          ALU.add, ALU.max, stats[:, h % PROBS, 0, q:q + 1])
                        last.then_inc(sem("a_max"), 1)
                        dve.wait_ge(sem("a_max"), st.at("a_max", b, h + 1))
                        v.tensor_scalar(stats[:, h % PROBS, 1, :], stats[:, h % PROBS, 0, :], -c["scale"], None,
                                        ALU.mult).then_inc(sem("a_negmax"), 1)

                    def invert(g):
                        dve.wait_ge(sem("a_exp"), st.at("a_exp", b, QUAD * (g + 1)))
                        dve.wait_ge(sem("a_pv"), st.since("a_pv", b, g - 1))
                        v.reciprocal(recip[:, :, :], sums[:, g % 2, :, :]).then_inc(sem("a_inv"), 1)
                        dve.wait_ge(sem("a_inv"), st.at("a_inv", b, g + 1))
                        v.tensor_copy(recips[:, g % 2, :, :], recip[:, :, :].rearrange("p q (j o) -> p (q j) o", o=1)
                                      .to_broadcast([P, QT * QUAD, SLOT])).then_inc(sem("a_recip"), 1)

                    def outputs(g):
                        dve.wait_ge(sem("a_pv"), st.at("a_pv", b, g + 1))
                        if g == 0:
                            dve.wait_ge(sem("a_y"), st.at("a_y", b))
                        v.tensor_copy(recipT[:, :], bank[6][:, T:2 * T]).then_inc(sem("a_rout"), 1)
                        dve.wait_ge(sem("a_rout"), st.at("a_rout", b, g + 1))
                        v.tensor_tensor(oT[:, g, :], bank[6][:, 0:T], recipT[:, :], ALU.mult)\
                            .then_inc(sem("a_oout"), 1)

                    if c["kinds"] == "mult":
                        times_mask(0)
                    for i in range(nh + QUAD + 2):
                        if c["kinds"] == "mult" and i + 1 < nh:
                            times_mask(i + 1)
                        if i < nh:
                            maxima(i)
                        if i % QUAD == 1 and 1 <= i // QUAD <= nh // QUAD:
                            invert(i // QUAD - 1)
                        if i % QUAD == 1 and i >= 2 * QUAD:
                            outputs(i // QUAD - 2)
                    dve.wait_ge(sem("a_resid"), st.at("a_resid", b, 1))
                    dve.wait_ge(sem("a_y"), st.at("a_y", b, 1))
                    v.tensor_tensor(ys, bank[7][:, :].rearrange("p (q d) -> p q d", q=QT), ys,
                                    ALU.add).then_inc(sem("a_yout"), 1)

            def mlp(n):
                st = S[f"m{n}"]
                with dve.Fori(0, B) as b:
                    xs = x_rows[:, bass.ds(b * QT, QT), :]
                    v.tensor_tensor(xs, xs, row2(f"m{n}"), ALU.add).then_inc(sem("m_resid"), 1)
                    dve.wait_ge(sem("m_resid"), st.at("m_resid", b, 1))
                    dve.wait_ge(sem("m_y"), st.at("m_y", b, 1))
                    for q in range(QT):
                        xq = x_rows[:, b * QT + q, :]
                        last = v.tensor_tensor(xq, bank[6 + q][:, 0:D], xq, ALU.add)
                    last.then_inc(sem("m_out"), 1)

            def wide(j):
                gs, st = S[f"g1{j}"], S[f"b1{j}"]
                v.memset(key_out[:, :], 0.0).then_inc(sem("e_bias"), 1)
                for q in range(B * QT):
                    last = v.tensor_tensor(x_rows[:, q, :], x_rows[:, q, :], row(f"o{j}"), ALU.add)
                last.then_inc(sem("e_bias"), 1)
                dve.wait_ge(sem("e_bias"), 2 * j)
                scale = P ** -0.5
                with dve.Fori(0, G1) as g:
                    with dve.Fori(0, B) as b:
                        u = g * B + b

                        def values(t):
                            dve.wait_ge(sem("b_proj"), st.at("b_proj", u, 2 + t))
                            dve.wait_ge(sem("b_pv"), st.at("b_pv", u))
                            dve.wait_ge(sem("c_bv"), gs.at("c_bv", g, 16))
                            v.tensor_tensor(v1[:, t, :], bank[V_BANK[t]][:, :], g_bv[:, :], ALU.add).then_inc(sem("b_v"), 1)

                        def maxima(h):
                            for q in range(QT):
                                dve.wait_ge(sem("b_scores"), st.at("b_scores", u, 2 * h + q + 1))
                                v.tensor_reduce(stats1[:, h % 2, 0, q:q + 1], bank[q][:, 0:K1], AX.X,
                                                ALU.max).then_inc(sem("b_rmax"), 1)
                            dve.wait_ge(sem("b_rmax"), st.at("b_rmax", u, 2 * h + 2))
                            v.tensor_scalar(stats1[:, h % 2, 1, :], stats1[:, h % 2, 0, :], -scale, None,
                                            ALU.mult).then_inc(sem("b_negmax"), 1)

                        def normalise(h):
                            dve.wait_ge(sem("b_exp"), st.at("b_exp", u, 2 * h + 2))
                            v.reciprocal(stats1[:, h % 2, 3, :], stats1[:, h % 2, 2, :]).then_inc(sem("b_recip"), 1)
                            dve.wait_ge(sem("b_recip"), st.at("b_recip", u, h + 1))
                            for q in range(QT):
                                s = probs1[:, h % 2, q, :]
                                last = v.tensor_scalar(s, s, stats1[:, h % 2, 3, q:q + 1], None, ALU.mult)
                            last.then_inc(sem("b_probs"), 1)
                            dve.wait_ge(sem("b_probs"), st.at("b_probs", u, h + 1))
                            for q in range(QT):
                                v.tensor_copy(p_key[:, b * QT + q, bass.ds(g * H1 + h, 1)],
                                              probs1[:, h % 2, q, T:K1])

                        def outputs(h):
                            dve.wait_ge(sem("b_pv"), st.at("b_pv", u, h + 1))
                            if h == 0:
                                dve.wait_ge(sem("b_y"), st.at("b_y", u))
                            v.tensor_copy(oT1[:, h, :], bank[6][:, 0:T]).then_inc(sem("b_oout"), 1)

                        values(0)
                        values(1)
                        maxima(0)
                        normalise(0)
                        maxima(1)
                        normalise(1)
                        outputs(0)
                        maxima(2)
                        normalise(2)
                        outputs(1)
                        maxima(3)
                        normalise(3)
                        outputs(2)
                        outputs(3)
                        dve.wait_ge(sem("b_y"), st.at("b_y", u, 1))
                        for q in range(QT):
                            xq = x_rows[:, b * QT + q, :]
                            last = v.tensor_tensor(xq, bank[[5, 7][q]][:, 0:D], xq, ALU.add)
                        last.then_inc(sem("b_yout"), 1)
                    dve.wait_ge(sem("c_key"), gs.at("c_key", g, 1))
                    v.tensor_tensor(key_out[:, :], bank[7][0:G1 * H1, 0:D], key_out[:, :],
                                    ALU.add).then_inc(sem("c_keyout"), 1)

            def learned_key(j):
                st = S[f"d1{j}"]
                with dve.Fori(0, B) as b:
                    dve.wait_ge(sem("d_t"), st.at("d_t", b))
                    v.tensor_copy(p_key_b[:, :, :], p_key[:, bass.ds(b * QT, QT), :]).then_inc(sem("d_copy"), 1)
                    dve.wait_ge(sem("d_y"), st.at("d_y", b, 1))
                    xs = x_rows[:, bass.ds(b * QT, QT), :]
                    v.tensor_tensor(xs, bank[7][:, :].rearrange("p (q d) -> p q d", q=QT), xs,
                                    ALU.add).then_inc(sem("d_yout"), 1)

            dve.wait_ge(sem("s_const"), 112)
            attention(SMALL[0], y_rows)
            norm("l0", "rms", y_rows, 1e-6)
            mlp(0)
            for j in (1, 2):
                norm(f"l1{j}", "ln", x_rows, 1e-5)
                wide(j)
                learned_key(j)
            norm("l1m", "ln", x_rows, 1e-5)
            mlp(1)
            norm("l21", "ln", x_rows, 1e-5)
            attention(SMALL[1], x_rows)
            norm("l22", "ln", x_rows, 1e-5)
            attention(SMALL[2], x_rows)
            norm("l23", "ln", x_rows, 1e-5)
            mlp(2)
            norm("l3t", "raw", x_rows)
            attention(SMALL[3], x_rows)
            norm("l3", "last", x_rows, 1e-6)

        @block.gpsimd
        def _(pool):
            nc.gpsimd.memset(half[:, :], -0.5).then_inc(sem("s_half"), 1)
            pool.wait_ge(sem("s_half"), 1)

            def one_head(c):
                st = S["a" + c["name"]]
                with pool.Fori(0, B) as b:
                    for h in range(c["heads"]):
                        if h == 0:
                            pool.wait_ge(sem("a_qout"), st.at("a_qout", b, KT))
                        pool.wait_ge(sem("a_scores"), st.since("a_scores", b, h - 3))
                        tile, mark, _, _ = c["head"](h)
                        nc.gpsimd.tensor_tensor(q_one[:, h % 4, :], qT[:, tile, :],
                                                marks[c["marks"]][:, mark:mark + 1].to_broadcast([P, T]),
                                                ALU.mult).then_inc(sem("a_qone"), 1)

            def power(name):
                st = S[name]
                with pool.Fori(0, B) as b:
                    pool.wait_ge(sem("l_eps"), st.at("l_eps", b, 1))
                    nc.gpsimd.tensor_tensor(rstd[:, :], ms[:, :], half[:, :], ALU.pow).then_inc(sem("l_rstd"), 1)

            pool.wait_ge(sem("s_const"), 112)
            one_head(SMALL[0])
            for name in ("l0", "l11", "l12", "l1m", "l21"):
                power(name)
            one_head(SMALL[1])
            power("l22")
            one_head(SMALL[2])
            power("l23")
            one_head(SMALL[3])
            power("l3")


def _layouts(i):
    import numpy as np

    def tiles(w):
        return w.reshape(w.shape[0] // P, P, w.shape[1]).transpose(1, 0, 2)

    def turned(x):
        return x.reshape(B, T, KT, P).transpose(0, 3, 2, 1)

    def vec(v):
        return v.reshape(-1, P).T

    def slots(wo, dh):
        n = wo.shape[0] // dh
        out = np.zeros((n, SLOT, D), wo.dtype)
        out[:, :dh] = wo.reshape(n, dh, D)
        return tiles(out.reshape(n * SLOT, D))

    def qkv(q, k, v):
        return np.stack([tiles(q), tiles(k), tiles(v)], 1)

    L0, L1, L2, L3 = ({n[9:]: np.asarray(w) for n, w in i.items() if n.startswith(f"L{b}_xattn_")} for b in range(4))
    o = {}
    x, c = np.asarray(i["x"]), np.asarray(i["ctx_2048"])
    o["x"] = x.reshape(B * QT, P, D).transpose(1, 0, 2)
    o["xT"], o["ctxT"] = turned(x), turned(c)
    o["ident"] = np.eye(P, dtype=np.float32)
    o["m16"] = np.repeat(np.eye(8, dtype=np.float32), 16, 0)
    o["m8"] = np.repeat(np.eye(16, dtype=np.float32), 8, 0)
    o["mask"] = np.asarray(i["mask_BxS2_ik0"]).reshape(B, 1, T)

    def rows2(m):
        return m.reshape(-1, QT, P, T).transpose(0, 2, 1, 3).reshape(-1, P, QT * T)

    o["mask_2"] = rows2(np.asarray(i["mask_1x1xSxS2_fc1"]))[0]
    o["mask_2c"] = rows2(np.asarray(i["mask_Bx1xSxS2_ff1"]))
    o["mask_3"] = rows2(np.asarray(i["mask_Bx1xSxS2_ff0"]))
    kv0, kvb0 = L0["kv_w"].reshape(D, D, 2), L0["kv_b"].reshape(D, 2)
    o["w_0"] = qkv(L0["q_w"], kv0[..., 0], kv0[..., 1])
    o["wo_0"] = slots(L0["out_w"], 16)
    wq2, wk2, wv2 = np.split(L2["w_qkv"], 3, 1)
    bq2, bk2, bv2 = np.split(L2["b_qkv"], 3)
    o["w_2"] = qkv(wq2, wk2, wv2)
    o["wo_2"] = slots(L2["w_ao"], 16)
    wkc, wvc = np.split(L2["w_kv"], 2, 1)
    bkc, bvc = np.split(L2["b_kv"], 2)
    o["w_2c"] = qkv(L2["w_q"], wkc, wvc)
    o["wo_2c"] = slots(L2["w_co"], 16)
    wq3 = L3["Wq"].reshape(D, 8, 4, 8).transpose(0, 2, 1, 3).reshape(D, D)
    bq3 = L3["bq"].reshape(8, 4, 8).transpose(1, 0, 2).reshape(D)
    wide3 = [np.concatenate([w, w] + [np.zeros_like(w)] * 2, 1) for w in (L3["Wk"], L3["Wv"])]
    o["w_3"] = qkv(wq3, *wide3)
    o["wo_3"] = slots(L3["Wo"], 8)
    for n, (a, b) in enumerate(((L0["mlp_w1"], L0["mlp_w2"]), (L1["w_fc1"], L1["w_fc2"]), (L2["w1"], L2["w2"]))):
        o[f"w1_{n}"], o[f"w2_{n}"] = tiles(a), tiles(b)
    heads = G1 * H1
    for j in (1, 2):
        g = [tiles(L1[n + str(j)]).reshape(P, KT, G1, H1 * P).transpose(2, 0, 1, 3) for n in ("wq", "wk", "wv")]
        o[f"g{j}"] = np.stack(g, 2)
        o[f"go{j}"] = L1[f"wo{j}"].reshape(G1, H1, P, D).transpose(0, 2, 1, 3)
        o[f"gbv{j}"] = L1[f"bv{j}"].reshape(G1, 1, H1 * P)
        kv = np.zeros((G1, P, H1, heads), np.float32)
        bias_v = L1[f"bias_v{j}"].reshape(G1, H1, P)
        for a in range(G1):
            for b in range(H1):
                kv[a, :, b, a * H1 + b] = bias_v[a, b]
        o[f"gkey{j}"] = kv
    bk3 = L3["bk"]
    cols = dict(q0=L0["q_b"], k0=kvb0[:, 0], b10=L0["mlp_b1"], post=L0["postnorm_w"], ln1s=L1["ln1_scale"],
                ln1o=L1["ln1_offset"], ln2s=L1["ln2_scale"], ln2o=L1["ln2_offset"], lnms=L1["ln_mlp_scale"],
                lnmo=L1["ln_mlp_offset"], b11=L1["b_fc1"], l2s1=L2["ln1_s"], l2b1=L2["ln1_b"], q2=bq2, k2=bk2,
                l2s2=L2["ln2_s"], l2b2=L2["ln2_b"], q2c=L2["b_q"], k2c=bkc, l2s3=L2["ln3_s"], l2b3=L2["ln3_b"],
                b12=L2["b1"], q3=bq3, k3=np.concatenate([bk3, bk3]), bq1=L1["bq1"], bk1=L1["bk1"],
                key1=L1["bias_k1"], bq2=L1["bq2"], bk2=L1["bk2"], key2=L1["bias_k2"])
    o["cols"] = np.concatenate([vec(cols[n].reshape(-1)) for n in COLS], 1)
    rows = dict(v0=kvb0[:, 1], o0=L0["out_b"], m0=L0["mlp_b2"], o1=L1["bo1"], o2=L1["bo2"], m1=L1["b_fc2"],
                v2=bv2, o2s=L2["b_ao"], v2c=bvc, o2c=L2["b_co"], m2=L2["b2"],
                v3=np.concatenate([L3["bv"], np.zeros(D - 64, np.float32)]), o3=L3["bo"],
                gamma=L3["gamma"], beta=L3["beta"])
    o["rows"] = np.concatenate([rows[n] for n in ROWS]).reshape(1, -1)
    return {n: np.ascontiguousarray(v) for n, v in o.items()}


def kernel(**inputs):
    import concourse.bacc as _bacc
    from concourse.bass_utils import run_bass_kernel_spmd as _run

    nc = _bacc.Bacc("TRN2", target_bir_lowering=False, num_devices=1)
    arrays, a = {}, {}
    for name, v in _layouts(inputs).items():
        arrays[f"in_{name}"] = v
        a[name] = nc.dram_tensor(f"in_{name}", v.shape, mybir.dt.from_np(v.dtype), kind="ExternalInput").ap()
    a["out"] = nc.dram_tensor("out_dram", (B, P, QT, D), F32, kind="ExternalOutput").ap()
    build(nc, a)
    r = _run(nc, [arrays], core_ids=[0]).results[0]["out_dram"]
    return r.transpose(0, 2, 1, 3).reshape(B, T, D)
```

```python
from contextlib import ExitStack

import concourse.bass as bass
from concourse import mybir

ALU = mybir.AluOpType
ACT = mybir.ActivationFunctionType
AX = mybir.AxisListType
F32 = mybir.dt.float32
I32 = mybir.dt.int32

P = 128
B = 4
T = 256
D = 256
KT = D // P
QT = T // P
F = 4 * D
FT = F // P
SLOT = 32
QUAD = P // SLOT
LAG = 3
PROBS = 4
BIG = -1.0e30
LOWEST = -3.0e38
KQ_BANK = [2, 2, 3, 2]
V_BANK = [3, 4]
G1, H1 = 4, 4
K1 = T + 1

COLS = ["q0", "k0", "b10", "post", "ln1s", "ln1o", "ln2s", "ln2o", "lnms", "lnmo", "b11",
        "l2s1", "l2b1", "q2", "k2", "l2s2", "l2b2", "q2c", "k2c", "l2s3", "l2b3", "b12", "q3", "k3",
        "bq1", "bk1", "key1", "bq2", "bk2", "key2"]
WIDTHS = dict.fromkeys(COLS, KT) | dict.fromkeys(["b10", "b11", "b12"], FT) | {"k3": 1} | dict.fromkeys(
    ["bq1", "bk1", "key1", "bq2", "bk2", "key2"], G1 * H1)
ROWS = ["v0", "o0", "m0", "o1", "o2", "m1", "v2", "o2s", "v2c", "o2c", "m2", "v3", "o3", "gamma", "beta"]
COL_AT = {n: sum(WIDTHS[m] for m in COLS[:i]) for i, n in enumerate(COLS)}
NCOL = sum(WIDTHS.values())


class Tally:

    def __init__(self, base, per):
        self.base, self.per = {n: base.get(n, 1) for n in per}, per

    def at(self, name, turn, k=0):
        return turn * self.per[name] + (self.base[name] + k)

    def since(self, name, turn, k):
        return self.at(name, turn, max(k, 0))


def small(name, **k):
    wide = dict(name=name, heads=16, dh=16, kv=KT, kinds="mult", qcol="q" + name, kcol="k" + name,
                head=lambda h: (h // 8, h % 8, h // 8, h), ktiles=2, marks="m16", vheads=16)
    return wide | k


SMALL = [
    small("0", kv=4, kinds="add", scale=1.0 / 16, vrow="v0", orow="o0", w=0, first="x"),
    small("2", scale=0.25, vrow="v2", orow="o2s", w=1, self_kv=True),
    small("2c", scale=0.25, vrow="v2c", orow="o2c", w=0),
    small("3", heads=32, dh=8, kinds="add", scale=8.0 ** -0.5, vrow="v3", orow="o3", w=1, marks="m8",
          vheads=8, ktiles=1,
          head=lambda h: (h % 4 // 2, h % 2 * 8 + h // 4, 0, h // 4)),
]


def build(nc, a):
    ctx = ExitStack()
    with ctx:
        def sb(name, shape, dt=F32):
            return ctx.enter_context(nc.sbuf_tensor(name, shape, dt))

        sems = {}

        def sem(name):
            if name not in sems:
                sems[name] = ctx.enter_context(nc.semaphore(name))
            return sems[name]

        bank = [ctx.enter_context(nc.psum_tensor(f"bank{i}", [P, 512], F32)) for i in range(8)]

        x_rows = sb("x_rows", [P, B * QT, D])
        y_rows = sb("y_rows", [P, B * QT, D])
        hT = sb("hT", [P, B, KT, T])
        ident = sb("ident", [P, P])
        marks = {"m16": sb("m16", [P, 8]), "m8": sb("m8", [P, 16])}
        cols = sb("cols", [P, NCOL])
        rows = sb("rows", [P, len(ROWS), D])
        half = sb("half", [P, B * QT])
        w_qkv = [sb(f"w_qkv{i}", [P, 3, KT, D]) for i in range(2)]
        w_o = [sb("w_o0", [P, 4, D]), sb("w_o1", [P, 8, D])]
        w_m1 = sb("w_m1", [P, KT, F])
        w_m2 = sb("w_m2", [P, FT, D])
        g_qkv = sb("g_qkv", [P, 3, KT, H1 * P])
        g_o = sb("g_o", [P, H1, D])
        g_bv = sb("g_bv", [P, H1 * P])
        g_key_v = sb("g_key_v", [P, H1, G1 * H1])
        kvT = sb("kvT", [P, KT, 2 * T])
        mask_i = sb("mask_i", [P, T], I32)
        mask_m = sb("mask_m", [P, QT * T])
        mask_a = sb("mask_a", [P, QT * T])
        qT = sb("qT", [P, KT, T])
        q_one = sb("q_one", [P, 4, T])
        kT = sb("kT", [P, 2, 2 * T])
        v_sb = sb("v_sb", [P, 4, 16, SLOT])
        probs = sb("probs", [P, PROBS, QT, 2 * T])
        pT = sb("pT", [P, 6, 4, T])
        oT = sb("oT", [P, 8, T])
        stats = sb("stats", [P, PROBS, 2, QT])
        sums = sb("sums", [P, 2, QT, QUAD])
        recips = sb("recips", [P, 2, QT * QUAD, SLOT])
        recip = sb("recip", [P, QT, QUAD])
        recipT = sb("recipT", [P, T])
        kT1 = sb("kT1", [P, 2, K1])
        qT1 = sb("qT1", [P, 2, T])
        v1 = sb("v1", [P, QT, H1 * P])
        probs1 = sb("probs1", [P, 2, QT, K1])
        pT1 = sb("pT1", [P, 2, QT, T])
        oT1 = sb("oT1", [P, H1, T])
        stats1 = sb("stats1", [P, 2, 4, QT])
        p_key = sb("p_key", [P, B * QT, G1 * H1])
        p_keyT = sb("p_keyT", [G1 * H1, B * T])
        key_out = sb("key_out", [G1 * H1, D])
        h1T = pT[:, 0:2, :, :].rearrange("p a t q -> p (a t) q")
        z = pT[:, 2:4, :, :].rearrange("p a t q -> p (a t) q")
        bn = sb("bn", [P, QT, 6])
        mv_b = sb("mv_b", [P, QT, 2])
        mv = sb("mv", [P, B * QT, 2])
        ms = sb("ms", [P, B * QT])
        rstd = sb("rstd", [P, B * QT])

        def col(name, i):
            return cols[:, COL_AT[name] + i:COL_AT[name] + i + 1]

        def row(name):
            return rows[:, ROWS.index(name), :]

        def row2(name):
            return rows[:, ROWS.index(name):ROWS.index(name) + 1, :].to_broadcast([P, QT, D])

        base = {}
        def stage(turns, per):
            t = Tally(base, per)
            for n, v in per.items():
                base[n] = base.get(n, 1) + turns * v
            return t

        def small_stage(c):
            nq, nh = c["heads"] // QUAD, c["heads"]
            return stage(B, dict(
                a_loaded=32 if c["name"] == "0" else 16, a_maskin=0 if c["name"] == "2" else 16,
                a_mask=1, a_proj=5 if c["kv"] == 4 else 3, a_qout=KT,
                a_kout=c["ktiles"], a_vout=c["kv"], a_qone=nh, a_scores=nh,
                a_masked=nh if c["kinds"] == "mult" else 0, a_max=nh, a_negmax=nh, a_exp=nh, a_inv=nq, a_recip=nq,
                a_t=nh, a_tout=nh, a_pv=nq, a_rout=nq, a_oout=nq, a_y=1, a_resid=1, a_yout=1))

        def norm_stage(kind):
            n, turned, final = int(kind != "raw"), int(kind != "last"), int(kind == "last")
            st = stage(1, dict(l_bn=B * n, l_aggr=B * n, l_mv=B * n, l_ms=int(kind == "rms"), l_eps=n, l_rstd=n,
                               l_z=B * n, l_t=B * turned, l_h=B // 2 * turned, l_hv=B // 2 * turned,
                               l_out=B * final, l_store=16 * B * final))
            st.per |= dict(l_bn=n, l_aggr=n, l_mv=n)
            return st

        def mlp_stage():
            return stage(B, dict(m_h=FT, m_gelu=FT, m_y=1, m_resid=1, m_out=1))

        def wide_stage():
            return stage(G1 * B, dict(b_loaded=16, b_proj=6, b_kq=4, b_v=2, b_scores=2 * H1, b_rmax=2 * H1, b_negmax=H1,
                                      b_exp=2 * H1, b_recip=H1, b_probs=H1, b_t=H1, b_tout=H1, b_pv=H1,
                                      b_oout=H1, b_y=1, b_yout=1))

        def group_stage():
            return stage(G1, dict(c_qkv=16, c_bv=16, c_o=32, c_key=1, c_keyout=1))

        def key_stage():
            return stage(1, dict(d_t=2, d_tout=1, d_tvout=1, d_y=B, d_yout=B))

        S = {}
        S["a0"] = small_stage(SMALL[0])
        S["l0"] = norm_stage("rms")
        S["m0"] = mlp_stage()
        for j in (1, 2):
            S[f"l1{j}"] = norm_stage("ln")
            S[f"g1{j}"] = group_stage()
            S[f"b1{j}"] = wide_stage()
            S[f"d1{j}"] = key_stage()
        S["l1m"] = norm_stage("ln")
        S["m1"] = mlp_stage()
        S["l21"] = norm_stage("ln")
        S["a2"] = small_stage(SMALL[1])
        S["l22"] = norm_stage("ln")
        S["a2c"] = small_stage(SMALL[2])
        S["l23"] = norm_stage("ln")
        S["m2"] = mlp_stage()
        S["l3t"] = norm_stage("raw")
        S["a3"] = small_stage(SMALL[3])
        S["l3"] = norm_stage("last")

        def end(st, name, turns=B):
            return S[st].base[name] + turns * S[st].per[name]

        block = ctx.enter_context(nc.Block())

        @block.sync
        def _(sp):
            def load(dst, src, name):
                sp.dma_start(dst, src).then_inc(sem(name), 16)

            load(ident[:, :], a["ident"], "s_const")
            load(marks["m16"][:, :], a["m16"], "s_const")
            load(marks["m8"][:, :], a["m8"], "s_const")
            load(cols[:, :], a["cols"], "s_const")
            load(hT[:, :, :, :], a["xT"].rearrange("b p k t -> p b k t"), "s_const")
            load(w_qkv[0][:, :, :, :], a["w_0"], "s_w0")
            load(w_o[0][:, :, :], a["wo_0"], "s_w0")
            load(rows[:, :, :].rearrange("p r d -> p (r d)"), a["rows"].to_broadcast([P, len(ROWS) * D]), "s_const")
            load(x_rows[:, :, :], a["x"], "s_const")

            for name in sorted(base):
                sp.sem_inc(sem(name), 1)

            def mlp_weights(n):
                load(w_m1[:, :, :], a[f"w1_{n}"], "s_wm")
                load(w_m2[:, :, :], a[f"w2_{n}"], "s_wm")

            def small_loads(c):
                st = S["a" + c["name"]]
                with sp.Fori(0, B) as b:
                    sp.wait_ge(sem("a_proj"), st.at("a_proj", b))
                    load(kvT[:, :, 0:T], hT[:, b, :, :] if "self_kv" in c else a["ctxT"][b], "a_loaded")
                    if c["name"] == "0":
                        load(kvT[:, :, T:2 * T], a["xT"][b], "a_loaded")
                        sp.wait_ge(sem("a_mask"), st.at("a_mask", b))
                        load(mask_i[:, :], a["mask"][b].to_broadcast([P, T]), "a_maskin")
                    elif c["name"] != "2":
                        sp.wait_ge(sem("a_max"), st.at("a_max", b))
                        load(mask_m[:, :], a["mask_" + c["name"]][b], "a_maskin")

            mlp_weights(0)
            small_loads(SMALL[0])
            sp.wait_ge(sem("a_proj"), end("a0", "a_proj"))
            for j in (1, 2):
                gs, bs = S[f"g1{j}"], S[f"b1{j}"]
                with sp.Fori(0, G1) as g:
                    sp.wait_ge(sem("b_proj"), bs.at("b_proj", g * B))
                    load(g_qkv[:, :, :, :], a[f"g{j}"][g], "c_qkv")
                    load(kvT[:, :, 0:T], a["ctxT"][0], "b_loaded")
                    sp.wait_ge(sem("b_v"), bs.at("b_v", g * B))
                    load(g_bv[:, :], a[f"gbv{j}"][g].to_broadcast([P, H1 * P]), "c_bv")
                    sp.wait_ge(sem("c_key"), gs.at("c_key", g))
                    load(g_o[:, :, :], a[f"go{j}"][g], "c_o")
                    load(g_key_v[:, :, :], a[f"gkey{j}"][g], "c_o")
                    with sp.Fori(1, B) as b:
                        sp.wait_ge(sem("b_proj"), bs.at("b_proj", g * B + b))
                        load(kvT[:, :, 0:T], a["ctxT"][b], "b_loaded")
                if j == 1:
                    sp.wait_ge(sem("m_y"), end("m0", "m_y"))
                    mlp_weights(1)
                    load(w_qkv[1][:, :, :, :], a["w_2"], "s_w1")
                    load(w_o[1][:, 0:4, :], a["wo_2"], "s_w1")
                    sp.wait_ge(sem("a_y"), end("a0", "a_y"))
                    load(w_qkv[0][:, :, :, :], a["w_2c"], "s_w0")
                    load(w_o[0][:, :, :], a["wo_2c"], "s_w0")
            sp.wait_ge(sem("a_max"), end("a0", "a_max"))
            load(mask_m[:, :], a["mask_2"], "s_m2")
            sp.wait_ge(sem("l_h"), end("l21", "l_h", 1))
            sp.wait_ge(sem("l_hv"), end("l21", "l_hv", 1))
            small_loads(SMALL[1])
            sp.wait_ge(sem("m_y"), end("m1", "m_y"))
            mlp_weights(2)
            sp.wait_ge(sem("a_y"), end("a2", "a_y"))
            load(w_qkv[1][:, :, :, :], a["w_3"], "s_w1")
            load(w_o[1][:, :, :], a["wo_3"], "s_w1")
            small_loads(SMALL[2])
            small_loads(SMALL[3])
            for b in range(B):
                sp.wait_ge(sem("l_out"), S["l3"].at("l_out", 0, b + 1))
                sp.dma_start(a["out"][b], z[:, b * QT:(b + 1) * QT, :]).then_inc(sem("l_store"), 16)
            sp.wait_ge(sem("l_store"), end("l3", "l_store", 1))

        @block.tensor
        def _(pe):
            mm = nc.tensor.matmul

            def norm(name, src=z):
                st = S[name]
                for b in range(B):
                    if src is z:
                        pe.wait_ge(sem("l_z"), st.at("l_z", 0, b + 1))
                    for q in range(QT):
                        for k in range(KT):
                            last = nc.tensor.transpose(bank[b][:, k * T + q * P:k * T + (q + 1) * P],
                                                       src[:, b * QT + q, k * P:(k + 1) * P], ident[:, :])
                    last.then_inc(sem("l_t"), 1)
                pe.wait_ge(sem("l_h"), end(name, "l_h", 1))
                pe.wait_ge(sem("l_hv"), end(name, "l_hv", 1))

            def attention(c, wn):
                st = S["a" + c["name"]]
                w, wo = w_qkv[c["w"]], w_o[c["w"]]
                nh, nkv = c["heads"], c["kv"]
                vw = c["vheads"] * c["dh"]
                pe.wait_ge(sem(f"s_w{c['w']}"), wn)
                with pe.Fori(0, B) as b:
                    pe.wait_ge(sem("a_max"), st.at("a_max", b))
                    for i in range(KT):
                        for k in range(KT):
                            last = mm(bank[0][:, i * T:(i + 1) * T], w[:, 0, k, i * P:(i + 1) * P],
                                      hT[:, b, k, :], start=(k == 0), stop=(k == KT - 1))
                    last.then_inc(sem("a_proj"), 1)
                    if "self_kv" not in c:
                        pe.wait_ge(sem("a_loaded"), st.at("a_loaded", b, st.per["a_loaded"]))
                    n = 1
                    for i in range(c["ktiles"]):
                        if nkv == 4:
                            out = bank[n][:, :]
                        else:
                            out = bank[n][:, i * T:(i + 1) * T]
                        for k in range(KT):
                            last = mm(out, w[:, 1, k, i * P:(i + 1) * P],
                                      hT[:, b, k, :] if "self_kv" in c else kvT[:, k, 0:nkv * P],
                                      start=(k == 0), stop=(k == KT - 1))
                        if nkv == 4 or i == c["ktiles"] - 1:
                            last.then_inc(sem("a_proj"), 1)
                            n += 1
                    if "self_kv" in c:
                        pe.wait_ge(sem("a_loaded"), st.at("a_loaded", b, 16))
                    pe.wait_ge(sem("a_yout"), st.at("a_yout", b))
                    for t in range(nkv):
                        vb = [bank[3], bank[7]][t // 2]
                        for k in range(KT):
                            last = mm(vb[:, t % 2 * T:t % 2 * T + vw], kvT[:, k, t * P:(t + 1) * P],
                                      w[:, 2, k, 0:vw], start=(k == 0), stop=(k == KT - 1))
                        if t % 2:
                            last.then_inc(sem("a_proj"), 1)

                    def scores(h):
                        pe.wait_ge(sem("a_qone"), st.at("a_qone", b, h + 1))
                        kt_ = c["head"](h)[2]
                        if h == 0:
                            pe.wait_ge(sem("a_kout"), st.at("a_kout", b, st.per["a_kout"]))
                        if h == (1 if nkv == 4 else 3):
                            pe.wait_ge(sem("a_vout"), st.at("a_vout", b, 2))
                        lag = 2 if nkv == 4 else 4
                        if h >= lag:
                            free = "a_masked" if c["kinds"] == "mult" else "a_max"
                            pe.wait_ge(sem(free), st.at(free, b, h - lag + 1))
                        for q in range(QT):
                            out = bank[h % 2 * 2 + q][:, :] if nkv == 4 else bank[h % 4][:, q * T:(q + 1) * T]
                            last = mm(out, q_one[:, h % 4, q * P:(q + 1) * P], kT[:, kt_, 0:nkv * P],
                                      start=True, stop=True)
                        last.then_inc(sem("a_scores"), 1)

                    def transposes(h):
                        pe.wait_ge(sem("a_exp"), st.at("a_exp", b, h + 1))
                        lag = 1 if nkv == 4 else 2
                        pe.wait_ge(sem("a_tout"), st.since("a_tout", b, h - lag + 1))
                        for t in range(nkv):
                            tb = bank[4 + t // 2] if nkv == 4 else bank[4 + h % 2]
                            for q in range(QT):
                                last = nc.tensor.transpose(tb[:, t % 2 * T + q * P:t % 2 * T + (q + 1) * P],
                                                           probs[:, h % PROBS, q, t * P:(t + 1) * P], ident[:, :])
                        last.then_inc(sem("a_t"), 1)

                    def outputs(g):
                        pe.wait_ge(sem("a_tout"), st.at("a_tout", b, QUAD * (g + 1)))
                        pe.wait_ge(sem("a_oout"), st.since("a_oout", b, g))
                        if g == 0:
                            pe.wait_ge(sem("a_vout"), st.at("a_vout", b, nkv))
                        for t in range(nkv):
                            for j in range(QUAD):
                                h = QUAD * g + j
                                last = mm(bank[6][SLOT * j:SLOT * (j + 1), 0:T],
                                          v_sb[:, t, c["head"](h)[3], :], pT[:, h % 6, t, :],
                                          start=(t == 0), stop=(t == nkv - 1), skip_group_check=True)
                        pe.wait_ge(sem("a_recip"), st.at("a_recip", b, g + 1))
                        for q in range(QT):
                            r = recips[:, g % 2, q * QUAD:(q + 1) * QUAD, :].rearrange("p j s -> p (j s)")
                            last = nc.tensor.transpose(bank[6][:, T + q * P:T + (q + 1) * P], r, ident[:, :])
                        last.then_inc(sem("a_pv"), 1)

                    ng = nh // QUAD

                    def project(g, q):
                        pe.wait_ge(sem("a_oout"), st.at("a_oout", b, g + 1))
                        if g == 0 and q == 1:
                            pe.wait_ge(sem("a_max"), st.at("a_max", b, nh))
                        return mm(bank[[7, 3][q]][:, 0:D], oT[:, g, q * P:(q + 1) * P], wo[:, g, :],
                                  start=(g == 0), stop=(g == ng - 1))

                    early = [(g, q) for q in range(QT) for g in range(ng - 2)]
                    for i in range(nh + QUAD + 1):
                        if i < nh:
                            scores(i)
                        if LAG <= i < nh + LAG:
                            transposes(i - LAG)
                        if i >= nh:
                            step, n = i - nh, QUAD
                            if i == nh:
                                outputs(ng - 2)
                            for g, q in early[step * len(early) // n:(step + 1) * len(early) // n]:
                                project(g, q)
                            if i == nh + QUAD:
                                project(ng - 2, 0)
                                outputs(ng - 1)
                                project(ng - 2, 1)
                        elif i >= 2 * QUAD and i % QUAD == 0:
                            outputs(i // QUAD - 2)
                    project(ng - 1, 0)
                    project(ng - 1, 1).then_inc(sem("a_y"), 1)

            def mlp(n):
                st = S[f"m{n}"]
                pe.wait_ge(sem("s_wm"), 32 * (n + 1))
                with pe.Fori(0, B) as b:
                    for f in range(FT + 2):
                        if f < FT:
                            pe.wait_ge(sem("m_gelu"), st.since("m_gelu", b, f - 3))
                            for k in range(KT):
                                last = mm(bank[f % 4][:, 0:T], w_m1[:, k, f * P:(f + 1) * P],
                                          hT[:, b, k, :], start=(k == 0), stop=(k == KT - 1))
                            last.then_inc(sem("m_h"), 1)
                        if f >= 2:
                            if f == 2:
                                pe.wait_ge(sem("m_out"), st.at("m_out", b))
                            pe.wait_ge(sem("m_gelu"), st.at("m_gelu", b, f - 1))
                            for q in range(QT):
                                last = mm(bank[6 + q][:, 0:D], h1T[:, f - 2, q * P:(q + 1) * P],
                                          w_m2[:, f - 2, :], start=(f == 2), stop=(f == FT + 1))
                    last.then_inc(sem("m_y"), 1)

            def wide(j):
                gs, st = S[f"g1{j}"], S[f"b1{j}"]
                with pe.Fori(0, G1) as g:
                    with pe.Fori(0, B) as b:
                        u = g * B + b
                        pe.wait_ge(sem("c_qkv"), gs.at("c_qkv", g, 16))
                        pe.wait_ge(sem("b_loaded"), st.at("b_loaded", u, 16))

                        def kq(h):
                            out = bank[KQ_BANK[h]]
                            if h == 0:
                                pe.wait_ge(sem("b_kq"), st.at("b_kq", u))
                            elif h == 1:
                                pe.wait_ge(sem("b_kq"), st.at("b_kq", u, 1))
                            elif h == 2:
                                pe.wait_ge(sem("b_v"), st.at("b_v", u, 1))
                            else:
                                pe.wait_ge(sem("b_kq"), st.at("b_kq", u, 2))
                            for k in range(KT):
                                mm(out[:, 0:T], g_qkv[:, 1, k, h * P:(h + 1) * P], kvT[:, k, 0:T],
                                   start=(k == 0), stop=(k == KT - 1))
                            for k in range(KT):
                                last = mm(out[:, T:2 * T], g_qkv[:, 0, k, h * P:(h + 1) * P], hT[:, b, k, :],
                                          start=(k == 0), stop=(k == KT - 1))
                            last.then_inc(sem("b_proj"), 1)

                        def values(t):
                            if t == 1:
                                pe.wait_ge(sem("b_tout"), st.at("b_tout", u))
                            for k in range(KT):
                                last = mm(bank[V_BANK[t]][:, :], kvT[:, k, t * P:(t + 1) * P], g_qkv[:, 2, k, :],
                                          start=(k == 0), stop=(k == KT - 1))
                            last.then_inc(sem("b_proj"), 1)

                        def scores(h):
                            pe.wait_ge(sem("b_kq"), st.at("b_kq", u, h + 1))
                            for q in range(QT):
                                pe.wait_ge(sem("b_exp"), st.since("b_exp", u, 2 * (h - 1) + q + 1))
                                mm(bank[q][:, 0:K1], qT1[:, h % 2, q * P:(q + 1) * P], kT1[:, h % 2, :],
                                   start=True, stop=True).then_inc(sem("b_scores"), 1)

                        def transposes(h):
                            pe.wait_ge(sem("b_probs"), st.at("b_probs", u, h + 1))
                            pe.wait_ge(sem("b_tout"), st.at("b_tout", u, h))
                            if h == 0:
                                pe.wait_ge(sem("b_v"), st.at("b_v", u, 2))
                            for t in range(QT):
                                for q in range(QT):
                                    last = nc.tensor.transpose(bank[4][:, t * T + q * P:t * T + (q + 1) * P],
                                                               probs1[:, h % 2, q, t * P:(t + 1) * P], ident[:, :])
                            last.then_inc(sem("b_t"), 1)

                        def outputs(h):
                            if h == 0:
                                pe.wait_ge(sem("b_v"), st.at("b_v", u, 2))
                            pe.wait_ge(sem("b_tout"), st.at("b_tout", u, h + 1))
                            pe.wait_ge(sem("b_oout"), st.at("b_oout", u, h))
                            for t in range(QT):
                                last = mm(bank[6][:, 0:T], v1[:, t, h * P:(h + 1) * P], pT1[:, h % 2, t, :],
                                          start=(t == 0), stop=(t == QT - 1))
                            last.then_inc(sem("b_pv"), 1)

                        def project(h):
                            pe.wait_ge(sem("b_oout"), st.at("b_oout", u, h + 1))
                            if h == 0:
                                pe.wait_ge(sem("b_yout"), st.at("b_yout", u))
                                pe.wait_ge(sem("c_keyout"), gs.at("c_keyout", g))
                                pe.wait_ge(sem("c_o"), gs.at("c_o", g, 32))
                            for q in range(QT):
                                last = mm(bank[[5, 7][q]][:, 0:D], oT1[:, h, q * P:(q + 1) * P], g_o[:, h, :],
                                          start=(h == 0), stop=(h == H1 - 1))
                            if h == H1 - 1:
                                last.then_inc(sem("b_y"), 1)

                        kq(0)
                        values(0)
                        values(1)
                        scores(0)
                        kq(1)
                        kq(2)
                        scores(1)
                        transposes(0)
                        kq(3)
                        outputs(0)
                        scores(2)
                        transposes(1)
                        project(0)
                        outputs(1)
                        scores(3)
                        transposes(2)
                        project(1)
                        outputs(2)
                        transposes(3)
                        project(2)
                        outputs(3)
                        project(3)
                    pe.wait_ge(sem("b_yout"), st.at("b_yout", (g + 1) * B))
                    for h in range(H1):
                        last = mm(bank[7][0:G1 * H1, 0:D], g_key_v[:, h, :], g_o[:, h, :],
                                  start=(h == 0), stop=(h == H1 - 1))
                    last.then_inc(sem("c_key"), 1)

            def learned_key(j):
                st = S[f"d1{j}"]
                pe.wait_ge(sem("c_keyout"), end(f"g1{j}", "c_keyout", G1))
                pe.wait_ge(sem("b_yout"), end(f"b1{j}", "b_yout", G1 * B))
                for q in range(B * QT):
                    last = nc.tensor.transpose(bank[4 + q // B][0:G1 * H1, q % B * P:(q % B + 1) * P],
                                               p_key[:, q, :], ident[:, :])
                    if q % B == B - 1:
                        last.then_inc(sem("d_t"), 1)
                for b in range(B):
                    if b == 0:
                        pe.wait_ge(sem("d_tout"), st.at("d_tout", 0, 1))
                    elif b == 2:
                        pe.wait_ge(sem("d_tvout"), st.at("d_tvout", 0, 1))
                    for q in range(QT):
                        last = mm(bank[b][:, q * D:(q + 1) * D], p_keyT[:, (b * QT + q) * P:(b * QT + q + 1) * P],
                                  key_out[:, :], start=True, stop=True)
                    last.then_inc(sem("d_y"), 1)

            pe.wait_ge(sem("s_const"), 112)
            attention(SMALL[0], 32)
            norm("l0")
            mlp(0)
            for j in (1, 2):
                norm(f"l1{j}")
                wide(j)
                learned_key(j)
            norm("l1m")
            mlp(1)
            norm("l21")
            attention(SMALL[1], 32)
            norm("l22")
            attention(SMALL[2], 64)
            norm("l23")
            mlp(2)
            pe.wait_ge(sem("m_out"), end("m2", "m_out"))
            norm("l3t", x_rows)
            attention(SMALL[3], 64)


        @block.scalar
        def _(act):
            def norm(name, scale=None, offset=None):
                st = S[name]
                for b in range(0, B, 2):
                    act.wait_ge(sem("l_t"), st.at("l_t", 0, b + 1))
                    for k in range(KT):
                        last = nc.scalar.activation(hT[:, b, k, :], bank[b][:, k * T:(k + 1) * T], ACT.Identity,
                                                    bias=col(offset, k) if offset else 0.0,
                                                    scale=col(scale, k) if scale else 1.0)
                    last.then_inc(sem("l_h"), 1)

            def attention(c):
                st = S["a" + c["name"]]
                nh, nkv = c["heads"], c["kv"]
                with act.Fori(0, B) as b:
                    for i in range(c["ktiles"]):
                        act.wait_ge(sem("a_proj"), st.at("a_proj", b, 2 + i if nkv == 4 else 2))
                        if i == 0:
                            act.wait_ge(sem("a_scores"), st.at("a_scores", b))
                        src = bank[1 + i][:, :] if nkv == 4 else bank[1][:, i * T:(i + 1) * T]
                        nc.scalar.activation(kT[:, i, 0:nkv * P], src, ACT.Identity,
                                             bias=col(c["kcol"], i)).then_inc(sem("a_kout"), 1)
                    for i in range(nh + LAG):
                        if i >= LAG:
                            h = i - LAG
                            act.wait_ge(sem("a_t"), st.at("a_t", b, h + 1))
                            act.wait_ge(sem("a_pv"), st.since("a_pv", b, (h - 6) // QUAD + 1))
                            for t in range(0, nkv, 2):
                                tb = bank[4 + t // 2] if nkv == 4 else bank[4 + h % 2]
                                last = nc.scalar.activation(pT[:, h % 6, t:t + 2, :].rearrange("p t q -> p (t q)"),
                                                            tb[:, :], ACT.Copy)
                            last.then_inc(sem("a_tout"), 1)
                        if i < nh:
                            act.wait_ge(sem("a_negmax"), st.at("a_negmax", b, i + 1))
                            if i % QUAD == 0:
                                act.wait_ge(sem("a_recip"), st.since("a_recip", b, i // QUAD - 1))
                            for q in range(QT):
                                s = probs[:, i % PROBS, q, 0:nkv * P]
                                last = nc.scalar.activation(s, s, ACT.Exp, bias=stats[:, i % PROBS, 1, q:q + 1],
                                                            scale=c["scale"], accum_out=sums[:, i // QUAD % 2, q, i % QUAD:i % QUAD + 1])
                            last.then_inc(sem("a_exp"), 1)

            def mlp(n, gelu):
                st = S[f"m{n}"]
                with act.Fori(0, B) as b:
                    act.wait_ge(sem("m_y"), st.at("m_y", b))
                    for f in range(FT):
                        act.wait_ge(sem("m_h"), st.at("m_h", b, f + 1))
                        nc.scalar.activation(h1T[:, f, :], bank[f % 4][:, 0:T], gelu,
                                             bias=col(f"b1{n}", f)).then_inc(sem("m_gelu"), 1)

            def wide(j):
                st = S[f"b1{j}"]
                scale = P ** -0.5
                with act.Fori(0, G1) as g:
                    with act.Fori(0, B) as b:
                        u = g * B + b

                        def kq(h):
                            act.wait_ge(sem("b_proj"), st.at("b_proj", u, [1, 4, 5, 6][h]))
                            act.wait_ge(sem("b_scores"), st.since("b_scores", u, 2 * (h - 1)))
                            src = bank[KQ_BANK[h]]
                            nc.scalar.activation(kT1[:, h % 2, 0:T], src[:, 0:T], ACT.Identity,
                                                 bias=cols[:, bass.ds(g * H1 + (COL_AT[f"bk{j}"] + h), 1)])
                            nc.scalar.activation(kT1[:, h % 2, T:K1], cols[:, bass.ds(g * H1 + (COL_AT[f"key{j}"] + h), 1)],
                                                 ACT.Copy)
                            nc.scalar.activation(qT1[:, h % 2, :], src[:, T:2 * T], ACT.Identity,
                                                 bias=cols[:, bass.ds(g * H1 + (COL_AT[f"bq{j}"] + h), 1)])\
                                .then_inc(sem("b_kq"), 1)

                        def exps(h):
                            act.wait_ge(sem("b_t"), st.since("b_t", u, h - 1))
                            act.wait_ge(sem("b_negmax"), st.at("b_negmax", u, h + 1))
                            for q in range(QT):
                                nc.scalar.activation(probs1[:, h % 2, q, :], bank[q][:, 0:K1], ACT.Exp,
                                                     bias=stats1[:, h % 2, 1, q:q + 1], scale=scale,
                                                     accum_out=stats1[:, h % 2, 2, q:q + 1]).then_inc(sem("b_exp"), 1)

                        def turned(h):
                            act.wait_ge(sem("b_t"), st.at("b_t", u, h + 1))
                            act.wait_ge(sem("b_pv"), st.since("b_pv", u, h - 1))
                            nc.scalar.activation(pT1[:, h % 2, :, :].rearrange("p t q -> p (t q)"), bank[4][:, :],
                                                 ACT.Copy).then_inc(sem("b_tout"), 1)

                        kq(0)
                        exps(0)
                        kq(1)
                        kq(2)
                        turned(0)
                        exps(1)
                        kq(3)
                        turned(1)
                        exps(2)
                        turned(2)
                        exps(3)
                        turned(3)

            def learned_key(j):
                st = S[f"d1{j}"]
                act.wait_ge(sem("d_t"), st.at("d_t", 0, 1))
                nc.scalar.activation(p_keyT[:, 0:2 * T], bank[4][0:G1 * H1, :], ACT.Copy).then_inc(sem("d_tout"), 1)

            act.wait_ge(sem("s_const"), 112)
            attention(SMALL[0])
            norm("l0", "post")
            mlp(0, ACT.Gelu_apprx_tanh)
            for j in (1, 2):
                norm(f"l1{j}", f"ln{j}s", f"ln{j}o")
                wide(j)
                learned_key(j)
            norm("l1m", "lnms", "lnmo")
            mlp(1, ACT.Gelu)
            norm("l21", "l2s1", "l2b1")
            attention(SMALL[1])
            norm("l22", "l2s2", "l2b2")
            attention(SMALL[2])
            norm("l23", "l2s3", "l2b3")
            mlp(2, ACT.Gelu_apprx_tanh)
            norm("l3t")
            attention(SMALL[3])

        def plain_wait(dve):
            dve.sem_inc(sem("e_step"), 1)

        @block.vector
        def _(dve):
            v = nc.vector

            def row_stats(name, b, src):
                st = S[name]
                plain_wait(dve)
                for q in range(QT):
                    last = v.bn_stats(bn[:, q, :], src[:, b * QT + q, :])
                last.then_inc(sem("l_bn"), 1)
                dve.wait_ge(sem("l_bn"), st.at("l_bn", b, 1))
                plain_wait(dve)
                for q in range(QT):
                    last = v.bn_aggr(mv_b[:, q, :], bn[:, q, :])
                last.then_inc(sem("l_aggr"), 1)
                dve.wait_ge(sem("l_aggr"), st.at("l_aggr", b, 1))
                rows_b = slice(b * QT, (b + 1) * QT) if isinstance(b, int) else bass.ds(b * QT, QT)
                v.tensor_copy(mv[:, rows_b, :], mv_b[:, :, :]).then_inc(sem("l_mv"), 1)

            def rstd_of(name, kind, eps):
                st = S[name]
                dve.wait_ge(sem("l_mv"), st.at("l_mv", B))
                if kind == "rms":
                    v.tensor_tensor(ms[:, :], mv[:, :, 0], mv[:, :, 0], ALU.mult).then_inc(sem("l_ms"), 1)
                    dve.wait_ge(sem("l_ms"), st.at("l_ms", 0, 1))
                    v.scalar_tensor_tensor(ms[:, :], ms[:, :], eps, mv[:, :, 1], ALU.add, ALU.add)\
                        .then_inc(sem("l_eps"), 1)
                else:
                    v.tensor_scalar(ms[:, :], mv[:, :, 1], eps, None, ALU.add).then_inc(sem("l_eps"), 1)
                dve.wait_ge(sem("l_rstd"), st.at("l_rstd", 0, 1))

            def norm(name, kind, src, eps=0.0, scale=None, offset=None):
                st = S[name]
                if kind != "raw":
                    rstd_of(name, kind, eps)
                    for b in range(B):
                        for q in range(b * QT, (b + 1) * QT):
                            if kind == "rms":
                                last = v.tensor_scalar(z[:, q, :], src[:, q, :], rstd[:, q:q + 1], None, ALU.mult)
                            else:
                                last = v.tensor_scalar(z[:, q, :], src[:, q, :], mv[:, q, 0:1], rstd[:, q:q + 1],
                                                       ALU.subtract, ALU.mult)
                        last.then_inc(sem("l_z"), 1)
                for b in range(1, B, 2):
                    dve.wait_ge(sem("l_t"), st.at("l_t", 0, b + 1))
                    for k in range(KT):
                        turned = bank[b][:, k * T:(k + 1) * T]
                        if offset:
                            last = v.tensor_scalar(hT[:, b, k, :], turned, col(scale, k), col(offset, k),
                                                   ALU.mult, ALU.add)
                        elif scale:
                            last = v.tensor_scalar(hT[:, b, k, :], turned, col(scale, k), None, ALU.mult)
                        else:
                            last = v.tensor_copy(hT[:, b, k, :], turned)
                    last.then_inc(sem("l_hv"), 1)

            def last_norm(name, eps):
                st = S[name]
                rstd_of(name, "ln", eps)
                for b in range(B):
                    for q in range(b * QT, (b + 1) * QT):
                        last = v.scalar_tensor_tensor(z[:, q, :], x_rows[:, q, :], mv[:, q, 0:1], row("gamma"),
                                                      ALU.subtract, ALU.mult)
                    last.then_inc(sem("l_z"), 1)
                    dve.wait_ge(sem("l_z"), st.at("l_z", 0, b + 1))
                    for q in range(b * QT, (b + 1) * QT):
                        last = v.scalar_tensor_tensor(z[:, q, :], z[:, q, :], rstd[:, q:q + 1], row("beta"),
                                                      ALU.mult, ALU.add)
                    last.then_inc(sem("l_out"), 1)

            def attention(c, dst, norm_name):
                st = S["a" + c["name"]]
                nh, nkv, dh = c["heads"], c["kv"], c["dh"]
                v.memset(v_sb[:, :, :, dh:SLOT], 0.0)
                if c["name"] == "0":
                    v.memset(mask_a[:, T:2 * T], 0.0)
                if c["name"] == "2":
                    dve.wait_ge(sem("s_m2"), 16)
                with dve.Fori(0, B) as b:
                    xs = x_rows[:, bass.ds(b * QT, QT), :]
                    ys = dst[:, bass.ds(b * QT, QT), :]
                    dve.wait_ge(sem("a_proj"), st.at("a_proj", b, 1))
                    for i in range(KT):
                        if i == 0:
                            dve.wait_ge(sem("a_qone"), st.at("a_qone", b))
                        v.tensor_scalar(qT[:, i, :], bank[0][:, i * T:(i + 1) * T], col(c["qcol"], i), None,
                                        ALU.add).then_inc(sem("a_qout"), 1)
                    if st.per["a_maskin"]:
                        dve.wait_ge(sem("a_maskin"), st.at("a_maskin", b, 16))
                    if c["name"] == "0":
                        ins = v.tensor_scalar(mask_a[:, 0:T], mask_i[:, :], 0.0, BIG, ALU.is_equal, ALU.mult)
                    elif c["kinds"] == "mult":
                        ins = v.tensor_scalar(mask_a[:, :], mask_m[:, :], -1.0, 10000.0 / c["scale"],
                                              ALU.add, ALU.mult)
                    else:
                        ins = v.tensor_scalar(mask_a[:, :], mask_m[:, :], 1.0 / c["scale"], None, ALU.mult)
                    ins.then_inc(sem("a_mask"), 1)
                    for t in range(nkv):
                        if t % 2 == 0:
                            dve.wait_ge(sem("a_proj"), st.at("a_proj", b, st.per["a_proj"] - nkv // 2 + t // 2 + 1))
                        vw = c["vheads"] * dh
                        v.tensor_tensor(
                            v_sb[:, t, 0:c["vheads"], 0:dh],
                            [bank[3], bank[7]][t // 2][:, t % 2 * T:t % 2 * T + vw].rearrange("p (h d) -> p h d", d=dh),
                            row(c["vrow"])[:, 0:vw].rearrange("p (h d) -> p h d", d=dh),
                            ALU.add).then_inc(sem("a_vout"), 1)
                    v.tensor_tensor(ys, xs, row2(c["orow"]), ALU.add).then_inc(sem("a_resid"), 1)

                    def times_mask(h):
                        dve.wait_ge(sem("a_scores"), st.at("a_scores", b, h + 1))
                        if h >= PROBS:
                            dve.wait_ge(sem("a_t"), st.at("a_t", b, h - PROBS + 1))
                        v.tensor_tensor(probs[:, h % PROBS, :, 0:T],
                                        bank[h % 4][:, :].rearrange("p (q t) -> p q t", q=QT),
                                        mask_m[:, :].rearrange("p (q t) -> p q t", q=QT),
                                        ALU.mult).then_inc(sem("a_masked"), 1)

                    def maxima(h):
                        if c["kinds"] == "mult":
                            dve.wait_ge(sem("a_masked"), st.at("a_masked", b, h + 1))
                        else:
                            dve.wait_ge(sem("a_scores"), st.at("a_scores", b, h + 1))
                            if h >= PROBS:
                                dve.wait_ge(sem("a_t"), st.at("a_t", b, h - PROBS + 1))
                        if h == 0:
                            dve.wait_ge(sem("a_mask"), st.at("a_mask", b, 1))
                        plain_wait(dve)
                        for q in range(QT):
                            if nkv == 4:
                                src, add = bank[h % 2 * 2 + q][:, :], mask_a[:, :]
                            else:
                                src, add = bank[h % 4][:, q * T:(q + 1) * T], mask_a[:, q * T:(q + 1) * T]
                            if c["kinds"] == "mult":
                                src = probs[:, h % PROBS, q, 0:T]
                            last = v.tensor_tensor_reduce(probs[:, h % PROBS, q, 0:nkv * P], src, add, 1.0, LOWEST,
                                                          ALU.add, ALU.max, stats[:, h % PROBS, 0, q:q + 1])
                        last.then_inc(sem("a_max"), 1)
                        dve.wait_ge(sem("a_max"), st.at("a_max", b, h + 1))
                        v.tensor_scalar(stats[:, h % PROBS, 1, :], stats[:, h % PROBS, 0, :], -c["scale"], None,
                                        ALU.mult).then_inc(sem("a_negmax"), 1)

                    def invert(g):
                        dve.wait_ge(sem("a_exp"), st.at("a_exp", b, QUAD * (g + 1)))
                        dve.wait_ge(sem("a_pv"), st.since("a_pv", b, g - 1))
                        v.reciprocal(recip[:, :, :], sums[:, g % 2, :, :]).then_inc(sem("a_inv"), 1)
                        dve.wait_ge(sem("a_inv"), st.at("a_inv", b, g + 1))
                        v.tensor_copy(recips[:, g % 2, :, :], recip[:, :, :].rearrange("p q (j o) -> p (q j) o", o=1)
                                      .to_broadcast([P, QT * QUAD, SLOT])).then_inc(sem("a_recip"), 1)

                    def outputs(g):
                        dve.wait_ge(sem("a_pv"), st.at("a_pv", b, g + 1))
                        if g == 0:
                            dve.wait_ge(sem("a_y"), st.at("a_y", b))
                        v.tensor_copy(recipT[:, :], bank[6][:, T:2 * T]).then_inc(sem("a_rout"), 1)
                        dve.wait_ge(sem("a_rout"), st.at("a_rout", b, g + 1))
                        v.tensor_tensor(oT[:, g, :], bank[6][:, 0:T], recipT[:, :], ALU.mult)\
                            .then_inc(sem("a_oout"), 1)

                    if c["kinds"] == "mult":
                        times_mask(0)
                    for i in range(nh + QUAD + 2):
                        if c["kinds"] == "mult" and i + 1 < nh:
                            times_mask(i + 1)
                        if i < nh:
                            maxima(i)
                        if i % QUAD == 1 and 1 <= i // QUAD <= nh // QUAD:
                            invert(i // QUAD - 1)
                        if i % QUAD == 1 and i >= 2 * QUAD:
                            outputs(i // QUAD - 2)
                    dve.wait_ge(sem("a_resid"), st.at("a_resid", b, 1))
                    dve.wait_ge(sem("a_y"), st.at("a_y", b, 1))
                    for q in range(QT):
                        yq = dst[:, b * QT + q, :]
                        last = v.tensor_tensor(yq, bank[[7, 3][q]][:, 0:D], yq, ALU.add)
                    last.then_inc(sem("a_yout"), 1)
                    dve.wait_ge(sem("a_yout"), st.at("a_yout", b, 1))
                    row_stats(norm_name, b, dst)

            def mlp(n, norm_name=None):
                st = S[f"m{n}"]
                with dve.Fori(0, B) as b:
                    xs = x_rows[:, bass.ds(b * QT, QT), :]
                    v.tensor_tensor(xs, xs, row2(f"m{n}"), ALU.add).then_inc(sem("m_resid"), 1)
                    dve.wait_ge(sem("m_resid"), st.at("m_resid", b, 1))
                    dve.wait_ge(sem("m_y"), st.at("m_y", b, 1))
                    for q in range(QT):
                        xq = x_rows[:, b * QT + q, :]
                        last = v.tensor_tensor(xq, bank[6 + q][:, 0:D], xq, ALU.add)
                    last.then_inc(sem("m_out"), 1)
                    if norm_name:
                        dve.wait_ge(sem("m_out"), st.at("m_out", b, 1))
                        row_stats(norm_name, b, x_rows)

            def wide(j):
                gs, st = S[f"g1{j}"], S[f"b1{j}"]
                v.memset(key_out[:, :], 0.0).then_inc(sem("e_bias"), 1)
                for q in range(B * QT):
                    last = v.tensor_tensor(x_rows[:, q, :], x_rows[:, q, :], row(f"o{j}"), ALU.add)
                last.then_inc(sem("e_bias"), 1)
                dve.wait_ge(sem("e_bias"), 2 * j)
                scale = P ** -0.5
                with dve.Fori(0, G1) as g:
                    with dve.Fori(0, B) as b:
                        u = g * B + b

                        def values(t):
                            dve.wait_ge(sem("b_proj"), st.at("b_proj", u, 2 + t))
                            dve.wait_ge(sem("b_pv"), st.at("b_pv", u))
                            dve.wait_ge(sem("c_bv"), gs.at("c_bv", g, 16))
                            v.tensor_tensor(v1[:, t, :], bank[V_BANK[t]][:, :], g_bv[:, :], ALU.add).then_inc(sem("b_v"), 1)

                        def maxima(h):
                            for q in range(QT):
                                dve.wait_ge(sem("b_scores"), st.at("b_scores", u, 2 * h + q + 1))
                                v.tensor_reduce(stats1[:, h % 2, 0, q:q + 1], bank[q][:, 0:K1], AX.X,
                                                ALU.max).then_inc(sem("b_rmax"), 1)
                            dve.wait_ge(sem("b_rmax"), st.at("b_rmax", u, 2 * h + 2))
                            v.tensor_scalar(stats1[:, h % 2, 1, :], stats1[:, h % 2, 0, :], -scale, None,
                                            ALU.mult).then_inc(sem("b_negmax"), 1)

                        def normalise(h):
                            dve.wait_ge(sem("b_exp"), st.at("b_exp", u, 2 * h + 2))
                            v.reciprocal(stats1[:, h % 2, 3, :], stats1[:, h % 2, 2, :]).then_inc(sem("b_recip"), 1)
                            dve.wait_ge(sem("b_recip"), st.at("b_recip", u, h + 1))
                            for q in range(QT):
                                s = probs1[:, h % 2, q, :]
                                last = v.tensor_scalar(s, s, stats1[:, h % 2, 3, q:q + 1], None, ALU.mult)
                            last.then_inc(sem("b_probs"), 1)
                            dve.wait_ge(sem("b_probs"), st.at("b_probs", u, h + 1))
                            for q in range(QT):
                                v.tensor_copy(p_key[:, b * QT + q, bass.ds(g * H1 + h, 1)],
                                              probs1[:, h % 2, q, T:K1])

                        def outputs(h):
                            dve.wait_ge(sem("b_pv"), st.at("b_pv", u, h + 1))
                            if h == 0:
                                dve.wait_ge(sem("b_y"), st.at("b_y", u))
                            v.tensor_copy(oT1[:, h, :], bank[6][:, 0:T]).then_inc(sem("b_oout"), 1)

                        values(0)
                        values(1)
                        maxima(0)
                        normalise(0)
                        maxima(1)
                        normalise(1)
                        outputs(0)
                        maxima(2)
                        normalise(2)
                        outputs(1)
                        maxima(3)
                        normalise(3)
                        outputs(2)
                        outputs(3)
                        dve.wait_ge(sem("b_y"), st.at("b_y", u, 1))
                        for q in range(QT):
                            xq = x_rows[:, b * QT + q, :]
                            last = v.tensor_tensor(xq, bank[[5, 7][q]][:, 0:D], xq, ALU.add)
                        last.then_inc(sem("b_yout"), 1)
                    dve.wait_ge(sem("c_key"), gs.at("c_key", g, 1))
                    v.tensor_tensor(key_out[:, :], bank[7][0:G1 * H1, 0:D], key_out[:, :],
                                    ALU.add).then_inc(sem("c_keyout"), 1)

            def learned_key(j, norm_name):
                st = S[f"d1{j}"]
                dve.wait_ge(sem("d_t"), st.at("d_t", 0, 2))
                v.tensor_copy(p_keyT[:, 2 * T:4 * T], bank[5][0:G1 * H1, :]).then_inc(sem("d_tvout"), 1)
                for b in range(B):
                    dve.wait_ge(sem("d_y"), st.at("d_y", 0, b + 1))
                    xs = x_rows[:, b * QT:(b + 1) * QT, :]
                    v.tensor_tensor(xs, bank[b][:, :].rearrange("p (q d) -> p q d", q=QT), xs,
                                    ALU.add).then_inc(sem("d_yout"), 1)
                    dve.wait_ge(sem("d_yout"), st.at("d_yout", 0, b + 1))
                    row_stats(norm_name, b, x_rows)

            dve.wait_ge(sem("s_const"), 112)
            attention(SMALL[0], y_rows, "l0")
            norm("l0", "rms", y_rows, 1e-6, "post")
            mlp(0, "l11")
            for j in (1, 2):
                norm(f"l1{j}", "ln", x_rows, 1e-5, f"ln{j}s", f"ln{j}o")
                wide(j)
                learned_key(j, ["l12", "l1m"][j - 1])
            norm("l1m", "ln", x_rows, 1e-5, "lnms", "lnmo")
            mlp(1, "l21")
            norm("l21", "ln", x_rows, 1e-5, "l2s1", "l2b1")
            attention(SMALL[1], x_rows, "l22")
            norm("l22", "ln", x_rows, 1e-5, "l2s2", "l2b2")
            attention(SMALL[2], x_rows, "l23")
            norm("l23", "ln", x_rows, 1e-5, "l2s3", "l2b3")
            mlp(2)
            norm("l3t", "raw", x_rows)
            attention(SMALL[3], x_rows, "l3")
            last_norm("l3", 1e-6)

        @block.gpsimd
        def _(pool):
            nc.gpsimd.memset(half[:, :], -0.5).then_inc(sem("s_half"), 1)
            pool.wait_ge(sem("s_half"), 1)

            def one_head(c):
                st = S["a" + c["name"]]
                with pool.Fori(0, B) as b:
                    for h in range(c["heads"]):
                        if h == 0:
                            pool.wait_ge(sem("a_qout"), st.at("a_qout", b, KT))
                        pool.wait_ge(sem("a_scores"), st.since("a_scores", b, h - 3))
                        tile, mark, _, _ = c["head"](h)
                        nc.gpsimd.tensor_tensor(q_one[:, h % 4, :], qT[:, tile, :],
                                                marks[c["marks"]][:, mark:mark + 1].to_broadcast([P, T]),
                                                ALU.mult).then_inc(sem("a_qone"), 1)

            def power(name):
                st = S[name]
                pool.wait_ge(sem("l_eps"), st.at("l_eps", 0, 1))
                nc.gpsimd.tensor_tensor(rstd[:, :], ms[:, :], half[:, :], ALU.pow).then_inc(sem("l_rstd"), 1)

            pool.wait_ge(sem("s_const"), 112)
            one_head(SMALL[0])
            for name in ("l0", "l11", "l12", "l1m", "l21"):
                power(name)
            one_head(SMALL[1])
            power("l22")
            one_head(SMALL[2])
            power("l23")
            one_head(SMALL[3])
            power("l3")


def _layouts(i):
    import numpy as np

    def tiles(w):
        return w.reshape(w.shape[0] // P, P, w.shape[1]).transpose(1, 0, 2)

    def turned(x):
        return x.reshape(B, T, KT, P).transpose(0, 3, 2, 1)

    def vec(v):
        return v.reshape(-1, P).T

    def slots(wo, dh):
        n = wo.shape[0] // dh
        out = np.zeros((n, SLOT, D), wo.dtype)
        out[:, :dh] = wo.reshape(n, dh, D)
        return tiles(out.reshape(n * SLOT, D))

    def qkv(q, k, v):
        return np.stack([tiles(q), tiles(k), tiles(v)], 1)

    L0, L1, L2, L3 = ({n[9:]: np.asarray(w) for n, w in i.items() if n.startswith(f"L{b}_xattn_")} for b in range(4))
    o = {}
    x, c = np.asarray(i["x"]), np.asarray(i["ctx_2048"])
    o["x"] = x.reshape(B * QT, P, D).transpose(1, 0, 2)
    o["xT"], o["ctxT"] = turned(x), turned(c)
    o["ident"] = np.eye(P, dtype=np.float32)
    o["m16"] = np.repeat(np.eye(8, dtype=np.float32), 16, 0)
    o["m8"] = np.repeat(np.eye(16, dtype=np.float32), 8, 0)
    o["mask"] = np.asarray(i["mask_BxS2_ik0"]).reshape(B, 1, T)

    def rows2(m):
        return m.reshape(-1, QT, P, T).transpose(0, 2, 1, 3).reshape(-1, P, QT * T)

    o["mask_2"] = rows2(np.asarray(i["mask_1x1xSxS2_fc1"]))[0]
    o["mask_2c"] = rows2(np.asarray(i["mask_Bx1xSxS2_ff1"]))
    o["mask_3"] = rows2(np.asarray(i["mask_Bx1xSxS2_ff0"]))
    kv0, kvb0 = L0["kv_w"].reshape(D, D, 2), L0["kv_b"].reshape(D, 2)
    o["w_0"] = qkv(L0["q_w"], kv0[..., 0], kv0[..., 1])
    o["wo_0"] = slots(L0["out_w"], 16)
    wq2, wk2, wv2 = np.split(L2["w_qkv"], 3, 1)
    bq2, bk2, bv2 = np.split(L2["b_qkv"], 3)
    o["w_2"] = qkv(wq2, wk2, wv2)
    o["wo_2"] = slots(L2["w_ao"], 16)
    wkc, wvc = np.split(L2["w_kv"], 2, 1)
    bkc, bvc = np.split(L2["b_kv"], 2)
    o["w_2c"] = qkv(L2["w_q"], wkc, wvc)
    o["wo_2c"] = slots(L2["w_co"], 16)
    wq3 = L3["Wq"].reshape(D, 8, 4, 8).transpose(0, 2, 1, 3).reshape(D, D)
    bq3 = L3["bq"].reshape(8, 4, 8).transpose(1, 0, 2).reshape(D)
    wide3 = [np.concatenate([w, w] + [np.zeros_like(w)] * 2, 1) for w in (L3["Wk"], L3["Wv"])]
    o["w_3"] = qkv(wq3, *wide3)
    o["wo_3"] = slots(L3["Wo"], 8)
    for n, (a, b) in enumerate(((L0["mlp_w1"], L0["mlp_w2"]), (L1["w_fc1"], L1["w_fc2"]), (L2["w1"], L2["w2"]))):
        o[f"w1_{n}"], o[f"w2_{n}"] = tiles(a), tiles(b)
    heads = G1 * H1
    for j in (1, 2):
        g = [tiles(L1[n + str(j)]).reshape(P, KT, G1, H1 * P).transpose(2, 0, 1, 3) for n in ("wq", "wk", "wv")]
        o[f"g{j}"] = np.stack(g, 2)
        o[f"go{j}"] = L1[f"wo{j}"].reshape(G1, H1, P, D).transpose(0, 2, 1, 3)
        o[f"gbv{j}"] = L1[f"bv{j}"].reshape(G1, 1, H1 * P)
        kv = np.zeros((G1, P, H1, heads), np.float32)
        bias_v = L1[f"bias_v{j}"].reshape(G1, H1, P)
        for a in range(G1):
            for b in range(H1):
                kv[a, :, b, a * H1 + b] = bias_v[a, b]
        o[f"gkey{j}"] = kv
    bk3 = L3["bk"]
    cols = dict(q0=L0["q_b"], k0=kvb0[:, 0], b10=L0["mlp_b1"], post=L0["postnorm_w"], ln1s=L1["ln1_scale"],
                ln1o=L1["ln1_offset"], ln2s=L1["ln2_scale"], ln2o=L1["ln2_offset"], lnms=L1["ln_mlp_scale"],
                lnmo=L1["ln_mlp_offset"], b11=L1["b_fc1"], l2s1=L2["ln1_s"], l2b1=L2["ln1_b"], q2=bq2, k2=bk2,
                l2s2=L2["ln2_s"], l2b2=L2["ln2_b"], q2c=L2["b_q"], k2c=bkc, l2s3=L2["ln3_s"], l2b3=L2["ln3_b"],
                b12=L2["b1"], q3=bq3, k3=np.concatenate([bk3, bk3]), bq1=L1["bq1"], bk1=L1["bk1"],
                key1=L1["bias_k1"], bq2=L1["bq2"], bk2=L1["bk2"], key2=L1["bias_k2"])
    o["cols"] = np.concatenate([vec(cols[n].reshape(-1)) for n in COLS], 1)
    rows = dict(v0=kvb0[:, 1], o0=L0["out_b"], m0=L0["mlp_b2"], o1=L1["bo1"], o2=L1["bo2"], m1=L1["b_fc2"],
                v2=bv2, o2s=L2["b_ao"], v2c=bvc, o2c=L2["b_co"], m2=L2["b2"],
                v3=np.concatenate([L3["bv"], np.zeros(D - 64, np.float32)]), o3=L3["bo"],
                gamma=L3["gamma"], beta=L3["beta"])
    o["rows"] = np.concatenate([rows[n] for n in ROWS]).reshape(1, -1)
    return {n: np.ascontiguousarray(v) for n, v in o.items()}


def kernel(**inputs):
    import concourse.bacc as _bacc
    from concourse.bass_utils import run_bass_kernel_spmd as _run

    nc = _bacc.Bacc("TRN2", target_bir_lowering=False, num_devices=1)
    arrays, a = {}, {}
    for name, v in _layouts(inputs).items():
        arrays[f"in_{name}"] = v
        a[name] = nc.dram_tensor(f"in_{name}", v.shape, mybir.dt.from_np(v.dtype), kind="ExternalInput").ap()
    a["out"] = nc.dram_tensor("out_dram", (B, P, QT, D), F32, kind="ExternalOutput").ap()
    build(nc, a)
    r = _run(nc, [arrays], core_ids=[0]).results[0]["out_dram"]
    return r.transpose(0, 2, 1, 3).reshape(B, T, D)
```
